# Optimizing a Trainium2 kernel written in Bass

```python
import numpy as np
import jax
import jax.numpy as jnp

def _softmax(x, axis=-1):
    return jax.nn.softmax(x, axis=axis)

def _gelu(x):
    return jax.nn.gelu(x, approximate=True)

def _silu(x):
    return jax.nn.silu(x)

def _sigmoid(x):
    return jax.nn.sigmoid(x)

def _layernorm(x, axis=-1, eps=1e-05):
    m = jnp.mean(x, axis=axis, keepdims=True)
    v = jnp.var(x, axis=axis, keepdims=True)
    return (x - m) / jnp.sqrt(v + eps)

def _scatter_add(tgt, idx, src, axis=0):
    return tgt.at[idx].add(src)

def _segment_sum(src, seg, n):
    return jax.ops.segment_sum(src, seg, n)
kernel_name = 'mk_flamingo_gated_d1_seqx_r4_c33102'

def setup_inputs(seed: int=0):
    np.random.seed(seed)
    _w = jnp.asarray

    def _rec_inputs():
        import jax
        import jax.numpy as jnp
        _rk = jax.random.key(seed)
        x = 7.22e-05 + 1 * jax.random.normal(jax.random.fold_in(_rk, 1), (4, 1024, 256), jnp.float32)
        _lenS = 1024 - jax.random.randint(jax.random.fold_in(_rk, 7), (4,), 0, max(1, 1024 // 4) + 1, jnp.int32)
        _lenS2 = 154 - jax.random.randint(jax.random.fold_in(_rk, 8), (4,), 0, max(1, 154 // 4) + 1, jnp.int32)
        _ctx_1024P = jax.random.normal(jax.random.fold_in(_rk, 11), (4, 16, 256), jnp.float32)
        _ctx_1024c = jax.random.dirichlet(jax.random.fold_in(_rk, 511), 0.3 * jnp.ones((16,), jnp.float32), (4, 154))
        _ctx_1024t = jnp.einsum('bsk,bkd->bsd', _ctx_1024c, _ctx_1024P)
        _ctx_1024t = _ctx_1024t * jax.lax.rsqrt(jnp.mean(jnp.square(_ctx_1024t)) + 1e-12) * 0.953939
        ctx_1024 = -0.000514642 + 1.00011 * (_ctx_1024t + 0.3 * jax.random.normal(jax.random.fold_in(_rk, 611), (4, 154, 256), jnp.float32))
        _g = jax.random.normal(jax.random.fold_in(_rk, 9001), (2, 1), jnp.float32)
        _g = jnp.sign(_g) * jnp.maximum(jnp.abs(_g), 1.0) + (_g == 0) * 1.0
        g_xattn = _g[0]
        g_ffn = _g[1]
        return (x, ctx_1024, g_xattn, g_ffn)
    x, ctx_1024, g_xattn, g_ffn = _rec_inputs()

    def _L0_xattn_setup():
        import jax, jax.numpy as jnp
        import numpy as np
        B, L_ENC, L_DEC, D = (16, 128, 128, 256)
        key = jax.random.key(seed)
        k1, k2, k3, k4, k5, k6 = jax.random.split(key, 6)
        encoder_hc = jax.random.normal(k1, (B, L_ENC, D), dtype=jnp.float32)
        decoder_hq = jax.random.normal(k2, (B, L_DEC, D), dtype=jnp.float32)
        w_sim = jax.random.normal(k3, (3 * D,), dtype=jnp.float32) * 0.02
        b_sim = jax.random.normal(k4, (1,), dtype=jnp.float32) * 0.02
        W_qv = jax.random.normal(k5, (4 * D, D), dtype=jnp.float32) * 0.02
        b_qv = jax.random.normal(k6, (D,), dtype=jnp.float32) * 0.02
        return {'encoder_hc': encoder_hc, 'decoder_hq': decoder_hq, 'w_sim': w_sim, 'b_sim': b_sim, 'W_qv': W_qv, 'b_qv': b_qv}
    _L0_xattn_all = _L0_xattn_setup()
    _L0_xattn_in = {k: v for k, v in _L0_xattn_all.items() if k in ('w_sim', 'b_sim', 'W_qv', 'b_qv')}
    del _L0_xattn_all

    def _L0_ffn_setup():
        import jax, jax.numpy as jnp
        import numpy as np
        BLOCK = 32
        W_BITS = 4
        ACT_BITS = 16

        def act_qdq(x):
            qmax = 2.0 ** (ACT_BITS - 1) - 1.0
            scale = jnp.maximum(jnp.max(jnp.abs(x)) / qmax, 1e-12)
            return jnp.clip(jnp.round(x / scale), -qmax - 1.0, qmax) * scale

        def fixed_qdq_u16(x):
            scale = 1.0 / 65536.0
            return jnp.clip(jnp.round(x / scale), 0.0, 65535.0) * scale

        def lpbq_dequant(w):
            O, I = w.shape
            qmax = 2.0 ** (W_BITS - 1) - 1.0
            wb = w.reshape(O, I // BLOCK, BLOCK)
            s = jnp.maximum(jnp.max(jnp.abs(wb), axis=-1, keepdims=True) / qmax, 1e-12)
            wq = jnp.clip(jnp.round(wb / s), -qmax - 1.0, qmax) * s
            return wq.reshape(O, I)
        key = jax.random.key(seed)
        k1, k2, k3, k4 = jax.random.split(key, 4)
        B, S, H, I = (2, 1024, 256, 768)
        x = jax.random.normal(k1, (B, S, H), jnp.float32)
        w_gate = jax.random.normal(k2, (I, H), jnp.float32) * 0.02
        w_up = jax.random.normal(k3, (I, H), jnp.float32) * 0.02
        w_down = jax.random.normal(k4, (H, I), jnp.float32) * 0.02
        return {'x': x, 'w_gate': w_gate, 'w_up': w_up, 'w_down': w_down}
    _L0_ffn_all = _L0_ffn_setup()
    _L0_ffn_in = {k: v for k, v in _L0_ffn_all.items() if k in ('w_gate', 'w_up', 'w_down')}
    del _L0_ffn_all
    return {'x': x, 'ctx_1024': ctx_1024, 'g_xattn': g_xattn, 'g_ffn': g_ffn, 'L0_xattn_w_sim': _L0_xattn_in['w_sim'], 'L0_xattn_b_sim': _L0_xattn_in['b_sim'], 'L0_xattn_W_qv': _L0_xattn_in['W_qv'], 'L0_xattn_b_qv': _L0_xattn_in['b_qv'], 'L0_ffn_w_gate': _L0_ffn_in['w_gate'], 'L0_ffn_w_up': _L0_ffn_in['w_up'], 'L0_ffn_w_down': _L0_ffn_in['w_down']}

def reference(x, ctx_1024, g_xattn, g_ffn, L0_xattn_w_sim, L0_xattn_b_sim, L0_xattn_W_qv, L0_xattn_b_qv, L0_ffn_w_gate, L0_ffn_w_up, L0_ffn_w_down):
    import jax
    import jax.numpy as jnp

    def _L0_xattn_ref(encoder_hc, decoder_hq, w_sim, b_sim, W_qv, b_qv):
        import jax, jax.numpy as jnp
        import numpy as np
        B, L_ENC, L_DEC, D = (16, 128, 128, 256)
        d = encoder_hc.shape[-1]
        w1, w2, w3 = (w_sim[:d], w_sim[d:2 * d], w_sim[2 * d:])
        Sim = (encoder_hc @ w1)[:, :, None] + (decoder_hq @ w2)[:, None, :] + jnp.einsum('bid,bjd->bij', encoder_hc * w3, decoder_hq) + b_sim[0]
        A = jax.nn.softmax(Sim, axis=2)
        hq_hat = jnp.einsum('bij,bjd->bid', A, decoder_hq)
        Batt = jax.nn.softmax(jnp.max(Sim, axis=2), axis=1)
        hc_bar = jnp.einsum('bi,bid->bd', Batt, encoder_hc)[:, None, :]
        hc_hat = jnp.broadcast_to(hc_bar, encoder_hc.shape)
        feats = jnp.concatenate([encoder_hc, hq_hat, encoder_hc * hq_hat, encoder_hc * hc_hat], axis=-1)
        hcq = feats @ W_qv + b_qv
        return hcq

    def _L0_ffn_ref(x, w_gate, w_up, w_down):
        import jax, jax.numpy as jnp
        import numpy as np
        BLOCK = 32
        W_BITS = 4
        ACT_BITS = 16

        def act_qdq(x):
            qmax = 2.0 ** (ACT_BITS - 1) - 1.0
            scale = jnp.maximum(jnp.max(jnp.abs(x)) / qmax, 1e-12)
            return jnp.clip(jnp.round(x / scale), -qmax - 1.0, qmax) * scale

        def fixed_qdq_u16(x):
            scale = 1.0 / 65536.0
            return jnp.clip(jnp.round(x / scale), 0.0, 65535.0) * scale

        def lpbq_dequant(w):
            O, I = w.shape
            qmax = 2.0 ** (W_BITS - 1) - 1.0
            wb = w.reshape(O, I // BLOCK, BLOCK)
            s = jnp.maximum(jnp.max(jnp.abs(wb), axis=-1, keepdims=True) / qmax, 1e-12)
            wq = jnp.clip(jnp.round(wb / s), -qmax - 1.0, qmax) * s
            return wq.reshape(O, I)
        x = act_qdq(x)
        up = act_qdq(x @ lpbq_dequant(w_up).T)
        gate = act_qdq(x @ lpbq_dequant(w_gate).T)
        sig = fixed_qdq_u16(jax.nn.sigmoid(gate))
        gate = act_qdq(gate * sig)
        o = act_qdq(gate * up)
        return o @ lpbq_dequant(w_down).T
    x = x + jnp.tanh(g_xattn[0]) * _L0_xattn_ref(_layernorm(x, axis=-1), ctx_1024, L0_xattn_w_sim, L0_xattn_b_sim, L0_xattn_W_qv, L0_xattn_b_qv)
    x = x + jnp.tanh(g_ffn[0]) * _L0_ffn_ref(_layernorm(x, axis=-1), L0_ffn_w_gate, L0_ffn_w_up, L0_ffn_w_down)
    return x

_drawn_inputs = setup_inputs


def setup_inputs(seed=0):
    import zlib

    import numpy as np

    out = dict(_drawn_inputs(seed))
    spreads = {}
    factors = {'L0_xattn_b_qv': 3.707}
    for name, (base, spread) in spreads.items():
        noise = np.random.default_rng([zlib.crc32(name.encode()), seed]).standard_normal(out[name].shape)
        drawn = base * np.exp(spread * noise) if base else spread * noise
        out[name] = jnp.asarray(drawn.astype(out[name].dtype))
    for name, factor in factors.items():
        out[name] = (out[name] * factor).astype(out[name].dtype)
    return out
```

```python
from contextlib import ExitStack

import concourse.bass as bass
from concourse import mybir
from concourse.alu_op_type import AluOpType as ALU

F32 = mybir.dt.float32
F32R = mybir.dt.float32r
F16 = mybir.dt.float16
BF16 = mybir.dt.bfloat16
I16 = mybir.dt.int16
U16 = mybir.dt.uint16
I32 = mybir.dt.int32
ACT = mybir.ActivationFunctionType
AX = mybir.AxisListType
RMAX = bass.bass_isa.ReduceOp.max
ds = bass.ds

P = 128
B, S, D = 4, 1024, 256
J = 154
JP = J // 2
FF = 768
KD = D // P
KF = FF // P
TOK = B * S
TB = S // P
NP = TB // 2
PT = 2 * P
HALF = TOK // 2
NU = 2 * KF
CH = 512
NC = TOK // CH
QB = 32
NB = FF * D // P // QB
WE = FF * D // P
QMAX = 32767.0
EPS = 1e-12
LN_EPS = 1e-5
COLS = 320
W_SCALE = 2.0 ** 11


def build(nc, x, ctx, g_xattn, g_ffn, w_sim, b_sim, w_qv, b_qv, w_gate, w_up, w_down, out):
    x1_dram = nc.dram_tensor("x1_scratch", (TOK, D), F32, kind="Internal").ap()

    base = -(-nc.sbuf_base // 64) * 64
    top = [base]

    def region(size):
        at = top[0]
        top[0] += -(-size // 32) * 32
        assert top[0] <= nc.sbuf_usable_end, (top[0], nc.sbuf_usable_end)
        return [at, at + size]

    def place(where, name, shape, dt, size_of={F32: 4, F32R: 4, I32: 4, F16: 2, BF16: 2, I16: 2, U16: 2}):
        n = size_of[dt]
        for k in shape[1:]:
            n *= k
        at = where[0]
        where[0] += -(-n // 32) * 32
        assert where[0] <= where[1], (name, where)
        return nc.alloc_sbuf_tensor_at(name, shape, dt, offset=at)

    r_hid = region(KF * TOK * 4)
    r_sgn = region(KF * TOK * 2)
    r_x = region(2 * KD * TOK * 2)
    r_wg = region(2 * KD * FF * 2)
    r_wu = region(2 * KD * FF * 2)
    r_wd = region(2 * KF * D * 2)
    r_tmp = region(12288)
    r_own = region(512 + 1280)

    def copy_of(r):
        return [r[0], r[1]]

    ident = place(r_own, "ident", [P, P], F32)
    cols = place(r_own, "cols", [P, COLS], F32)
    used = [0]

    def col(n=1):
        used[0] += n
        assert used[0] <= COLS
        return cols[:, used[0] - n:used[0]]

    hid = place(copy_of(r_hid), "hid", [P, KF, TOK], F32)
    gq = place(copy_of(r_sgn), "gq", [P, KF, TOK], I16)
    a = copy_of(r_x)
    xh = place(a, "xh", [P, KD, TOK], F16)
    xl = place(a, "xl", [P, KD, TOK], F16)
    a = copy_of(r_wg)
    wgh = place(a, "wgh", [P, KD, FF], F16)
    wgl = place(a, "wgl", [P, KD, FF], F16)
    a = copy_of(r_wu)
    wuh = place(a, "wuh", [P, KD, FF], F16)
    wul = place(a, "wul", [P, KD, FF], F16)
    a = copy_of(r_wd)
    wdh = place(a, "wdh", [P, KF, D], F16)
    wdl = place(a, "wdl", [P, KF, D], F16)
    a = copy_of(r_tmp)
    ag = place(a, "ag", [P, 2, HALF], I16)
    sq = place(a, "sq", [P, HALF], U16)
    a = copy_of(r_tmp)
    au = place(a, "au", [P, 2, HALF], I16)
    pq = [place(a, "pq0", [P, HALF], I16), place(copy_of(r_wg), "pq1", [P, HALF], I16)]
    oq = place(copy_of(r_tmp), "oq", [P, 2, KF, CH], I16)
    a = copy_of(r_x)
    oh = place(a, "oh", [P, 2, KF, CH], F16)
    ol = place(a, "ol", [P, 2, KF, CH], F16)
    xo = place([r_wg[0], r_wu[1]], "xo", [P, 2, 4, D], F32)

    a = copy_of(r_sgn)
    yT = place(a, "yT", [P, KD, TOK], F32)
    xqi = place(copy_of(a), "xqi", [P, 2, KD, CH], I16)
    hTf = place(a, "hTf", [P, KD, S], F32)
    ath = place(a, "ath", [JP, 2, CH], F32R)
    atl = place(a, "atl", [JP, 2, CH], F32R)
    a = copy_of(r_hid)
    xa = place(a, "xa", [P, B * TB, D], F32)
    hth = place(a, "hth", [P, KD, S], F32R)
    htl = place(a, "htl", [P, KD, S], F32R)
    wmid = place(copy_of(a), "wmid", [P, 2 * KD, D], F32)
    hqh = place(a, "hqh", [P, KD, S], F32R)
    hql = place(a, "hql", [P, KD, S], F32R)
    prh = place(a, "prh", [P, KD, S], F32R)
    prl = place(a, "prl", [P, KD, S], F32R)
    wmh = place(a, "wmh", [P, 2 * KD, D], F32R)
    wml = place(a, "wml", [P, 2 * KD, D], F32R)
    weh = place(a, "weh", [P, KD, D], F32R)
    wel = place(a, "wel", [P, KD, D], F32R)
    w0 = place(a, "w0", [P, KD, D], F32)
    w3 = place(a, "w3", [P, KD, D], F32)
    a = copy_of(r_x)
    wr = place(a, "wr", [P, 3, WE], F32)
    h = place(a, "h", [P, TB, D], F32)
    wqi = place(a, "wqi", [P, WE], I16)
    wsc = place(a, "wsc", [P, 3, NB], F32)
    wri = place(a, "wri", [P, 3, NB], F32)
    a = [r_wg[0], r_wd[1]]
    cx = place(a, "cx", [JP, 2, D], F32)
    cxh = place(a, "cxh", [JP, 2, D], F32R)
    cxl = place(a, "cxl", [JP, 2, D], F32R)
    cxT = place(a, "cxT", [P, KD, J], F32)
    cpf = place(a, "cpf", [P, KD, J], F32)
    cph = place(a, "cph", [P, KD, J], F32R)
    cpl = place(a, "cpl", [P, KD, J], F32R)
    cbi = place(a, "cbi", [P, J], F32)
    wef = place(a, "wef", [P, KD, D], F32)
    w2b = place(a, "w2b", [P, KD, P], F32)
    ones = place(a, "ones", [P, P], F32)
    diag = place(a, "diag", [P, P], F32)
    row = place(a, "row", [1, D + 3], F32)
    wcol = place(a, "wcol", [P, 3 * KD], F32)
    a = copy_of(r_tmp)
    yb = place(a, "yb", [P, 2, 2, D], F32)
    sc = place(a, "sc", [P, 2, 2, J], F32)
    pf = place(a, "pf", [P, 2, CH], F32)
    tgb = place(a, "tgb", [P, D], F32)
    st = place(a, "st", [P, TB, 6], F32)

    mv = col(2 * B * TB).rearrange("p (t s) -> p t s", s=2)
    mvb = col(2 * TB).rearrange("p (t s) -> p t s", s=2)
    rstd = col(B * TB)
    mhalf = col(B * TB)
    mv2 = col(4).rearrange("p (t s) -> p t s", s=2)
    vp2, rstd2 = col(2), col(2)
    rm, nm = col(TB), col(TB)
    rs, ri = col(TB), col(TB)
    eb = col(TB)
    ymx = col(B * NP)
    gmx, umx, pmx, omx = col(NU), col(NU), col(NU), col(NU)
    c_m1, c_ngm, c_es, c_rs, c_hc = col(), col(), col(), col(), col(KD)
    c_t2 = col(2)
    c_tx, c_tf = c_t2[:, 0:1], c_t2[:, 1:2]
    c_bs = col()
    c_sm, c_sa, c_pw, c_wt, c_dn = col(3), col(3), col(3), col(3), col(3)
    c_loc, c_all = col(5), col(5)
    c_sx, c_ix, c_kg, c_kgq, c_ku, c_kuq = (col() for _ in range(6))
    c_sg, c_rg, c_cg, c_kp, c_kpq = (col() for _ in range(5))
    c_su, c_ru, c_cu, c_sp, c_rp, c_cp = (col() for _ in range(6))
    c_ko, c_so, c_ro, c_co, c_ft, c_fin = (col() for _ in range(6))

    ps = [nc.alloc_psum_tensor(f"ps{i}", [P, 4, 512], F32) for i in range(2)]
    tb_bank, sb_bank, ab_bank, yb_bank = ps[0][:, 0, :], ps[0][:, 1, :], ps[0][:, 2, :], ps[0][:, 3, :]
    hq_bank = [ps[1][:, 0, :], ps[1][:, 1, :]]
    f_bank = [ps[1][:, 2, :], ps[1][:, 3, :]]

    x_v = x.rearrange("b (t p) d -> p (b t) d", p=P)
    ctx_v = ctx.rearrange("b (k p) d -> b p k d", p=JP)
    wqv_v = w_qv.rearrange("(k p) n -> p k n", p=P)
    wsim_v = w_sim.rearrange("(k p) -> p k", p=P)
    x1_v = x1_dram.rearrange("(t p) d -> p t d", p=P)
    out_v = out.rearrange("b (t p) d -> p (b t) d", p=P)

    with ExitStack() as stack:
        def sem(name):
            return stack.enter_context(nc.semaphore(name))

        x0_in, xr_in, cx_in, small_in, wqv_in, wffn_in = map(sem, ("x0_in", "xr_in", "cx_in", "small_in", "wqv_in", "wffn_in"))
        x1_out, xo_in, xo_in1, out_out = map(sem, ("x1_out", "xo_in", "xo_in1", "out_out"))
        const_a, ident_rdy, mhalf_rdy, ones_rdy, rows_ps, tanh_rdy, tgb_rdy, w2b_rdy, wmh_rdy, wml_rdy = map(
            sem, ("const_a", "ident_rdy", "mhalf_rdy", "ones_rdy", "rows_ps", "tanh_rdy", "tgb_rdy", "w2b_rdy", "wmh_rdy", "wml_rdy"))
        bn_done, agg_done, mv_done, vp_done, rstd_rdy, h_rdy, xb_rdy = map(sem, ("bn_done", "agg_done", "mv_done", "vp_done", "rstd_rdy", "h_rdy", "xb_rdy"))
        cxT_ps, cxT_rdy, cbi_ps, cbi_rdy, cpf_rdy, cph_rdy, cp_rdy, cxh_rdy, cx_rdy = map(
            sem, ("cxT_ps", "cxT_rdy", "cbi_ps", "cbi_rdy", "cpf_rdy", "cph_rdy", "cp_rdy", "cxh_rdy", "cx_rdy"))
        hT_ps, hTf_rdy, hth_rdy, htl_rdy = map(sem, ("hT_ps", "hTf_rdy", "hth_rdy", "htl_rdy"))
        sc_ps, sc_rdy, nm_rdy, exp_rdy, ri_rdy, a_rdy = map(sem, ("sc_ps", "sc_rdy", "nm_rdy", "exp_rdy", "ri_rdy", "a_rdy"))
        at_ps, ath_rdy, at_rdy = map(sem, ("at_ps", "ath_rdy", "at_rdy"))
        hq_ps, hqh_rdy, hql_rdy, pf_rdy, prh_rdy, prl_rdy = map(sem, ("hq_ps", "hqh_rdy", "hql_rdy", "pf_rdy", "prh_rdy", "prl_rdy"))
        m1_rdy, diag_rdy, m_ps, ngm_rdy, eb_rdy, hc_ps, crs_rdy, hc_rdy = map(
            sem, ("m1_rdy", "diag_rdy", "m_ps", "ngm_rdy", "eb_rdy", "hc_ps", "crs_rdy", "hc_rdy"))
        wef_rdy, weh_rdy, we_rdy = map(sem, ("wef_rdy", "weh_rdy", "we_rdy"))
        f_ps, x1_rdy, bn2_done, mv2_done, vp2_done, rstd2_rdy, y_rdy, ym_done, yT_ps, yT_rdy = map(
            sem, ("f_ps", "x1_rdy", "bn2_done", "mv2_done", "vp2_done", "rstd2_rdy", "y_rdy", "ym_done", "yT_ps", "yT_rdy"))
        wmax_a, wscale_a, wchain, wall_rdy, wq_rdy, wqi_rdy, wn_rdy, wt_ps, wth_rdy, wt_rdy = map(
            sem, ("wmax_a", "wscale_a", "wchain", "wall_rdy", "wq_rdy", "wqi_rdy", "wn_rdy", "wt_ps", "wth_rdy", "wt_rdy"))
        loc_rdy, all_rdy, chain, scales = map(sem, ("loc_rdy", "all_rdy", "chain", "scales"))
        xqi_rdy, xh_rdy, xq_rdy, unit_ps, gm_done = map(sem, ("xqi_rdy", "xh_rdy", "xq_rdy", "unit_ps", "gm_done"))
        half_free = [sem("half0_free"), sem("half1_free")]
        gq_rdy, ag_rdy, sig_rdy, sq_rdy, p_rdy, pq_rdy, au_rdy, o_rdy = map(
            sem, ("gq_rdy", "ag_rdy", "sig_rdy", "sq_rdy", "p_rdy", "pq_rdy", "au_rdy", "o_rdy"))
        oqa_rdy, sgn_rdy, oqs_rdy, oh_rdy, os_rdy, dn_ps, fin_rdy = map(
            sem, ("oqa_rdy", "sgn_rdy", "oqs_rdy", "oh_rdy", "os_rdy", "dn_ps", "fin_rdy"))

        passed = sem("passed")

        block = stack.enter_context(nc.Block())

        def unit(t, k, hf):
            return t[:, ds(k, 1), hf * HALF:(hf + 1) * HALF].rearrange("p a n -> p (a n)")

        def ps_half(hf):
            return ps[hf][:].rearrange("p a n -> p (a n)")

        w_bank = [tb_bank, sb_bank, ab_bank]

        def w_part(m, q, low):
            if m == 2:
                return (wdh, wdl)[low][:, 2 * q:2 * q + 2, :].rearrange("p k n -> p (k n)")
            return ((wgh, wgl), (wuh, wul))[m][low][:, :, q * D:(q + 1) * D]

        def w_seen(m, q):
            return w_bank[q] if m == 2 else w_bank[q].rearrange("p (k n) -> p k n", k=KD)

        def ge(eng, s, n):
            if not isinstance(n, int) or n > 0:
                eng.wait_ge(s, n)

        def plain(eng):
            eng.sem_inc(passed, 1)

        @block.sync
        def _(sp):
            for t in range(0, TB, 2):
                sp.dma_start(xa[:, t:t + 2, :], x_v[:, t:t + 2, :]).then_inc(x0_in, 16)
            sp.dma_start(cx[:], ctx_v[0]).then_inc(cx_in, 16)
            sp.dma_start(wmid[:], wqv_v[:, KD:3 * KD, :]).then_inc(wqv_in, 16)
            sp.dma_start(w0[:], wqv_v[:, 0:KD, :]).then_inc(wqv_in, 16)
            sp.dma_start(w3[:], wqv_v[:, 3 * KD:4 * KD, :]).then_inc(wqv_in, 16)
            for b in range(1, B):
                sp.dma_start(xa[:, b * TB:(b + 1) * TB, :], x_v[:, b * TB:(b + 1) * TB, :]).then_inc(xr_in, 16)
            for m, w in enumerate((w_gate, w_up)):
                sp.dma_start(wr[:, m, :].rearrange("p (k n) -> p k n", n=D),
                             w.rearrange("(k p) n -> p k n", p=P)).then_inc(wffn_in, 16)
            sp.dma_start(wr[:, 2, :].rearrange("p (k n) -> p k n", n=FF),
                         w_down.rearrange("(k p) n -> p k n", p=P)).then_inc(wffn_in, 16)
            with sp.Fori(1, B) as b:
                sp.wait_ge(cxT_ps, b)
                sp.wait_ge(cx_rdy, b)
                sp.dma_start(cx[:], ctx_v[ds(b, 1)].rearrange("b p k d -> p (b k) d")).then_inc(cx_in, 16)
            with sp.Fori(0, B) as b:
                sp.wait_ge(x1_rdy, b * NP + NP)
                sp.dma_start(x1_v[:, ds(b * TB, TB), :], xa[:, ds(b * TB, TB), :]).then_inc(x1_out, 16)
            sp.wait_ge(x1_out, 16 * B)
            sp.wait_ge(unit_ps, 3 * NU)
            sp.wait_ge(o_rdy, NU)
            sp.dma_start(xo[:, 0], x1_v[:, 0:4, :]).then_inc(xo_in, 16)
            sp.dma_start(xo[:, 1], x1_v[:, 4:8, :]).then_inc(xo_in1, 16)

            def store(c2, par):
                sp.wait_ge(fin_rdy, c2 * 2 + par + 1)
                sp.dma_start(out_v[:, ds(c2 * 8 + par * 4, 4), :], xo[:, par]).then_inc(out_out, 16)

            with sp.Fori(0, NC // 2 - 1) as c2:
                for par in range(2):
                    store(c2, par)
                    sp.wait_ge(out_out, c2 * 32 + par * 16 + 16)
                    sp.dma_start(xo[:, par], x1_v[:, ds(c2 * 8 + 8 + par * 4, 4), :]).then_inc((xo_in, xo_in1)[par], 16)
            for par in range(2):
                store(NC // 2 - 1, par)
            sp.wait_ge(out_out, 16 * NC)

        @block.gpsimd
        def _(pool):
            pool.memset(ident[:], 0.0).then_inc(const_a, 1)
            pool.memset(mhalf, -0.5).then_inc(mhalf_rdy, 1)
            pool.memset(ones[:], 1.0).then_inc(ones_rdy, 1)
            pool.wait_ge(const_a, 1)
            pool.affine_select(out=ident[:], in_=ident[:], compare_op=ALU.not_equal, fill=1.0, base=0,
                               pattern=[[-1, P]], channel_multiplier=1).then_inc(ident_rdy, 1)

            def row_std(n, lo, hi):
                pool.wait_ge(vp_done, n)
                pool.tensor_tensor(rstd[:, lo:hi], rstd[:, lo:hi], mhalf[:, lo:hi], ALU.pow).then_inc(rstd_rdy, 1)

            def body(b, scores, project):
                f = b - 1
                for s in range(NP):
                    if scores:
                        pool.wait_ge(hth_rdy, b * NP + s + 1)
                        pool.wait_ge(hTf_rdy, b * NP + s + 1)
                        q = slice(s * PT, (s + 1) * PT)
                        pool.tensor_tensor(htl[:, :, q], hTf[:, :, q], hth[:, :, q].bitcast(F32), ALU.subtract).then_inc(htl_rdy, 1)
                    if project:
                        pool.wait_ge(vp2_done, f * NP + s + 1)
                        ge(pool, y_rdy, f * NP + s)
                        pool.tensor_tensor(rstd2, vp2, mhalf[:, 0:2], ALU.pow).then_inc(rstd2_rdy, 1)
                    if scores:
                        pool.wait_ge(h_rdy, b * NP + s + 1)
                        t = ds(b * TB + 2 * s, 2)
                        pool.tensor_tensor(xa[:, t, :], xa[:, t, :], tgb[:].unsqueeze(1).broadcast_to([P, 2, D]), ALU.add).then_inc(xb_rdy, 1)
                if scores:
                    for hf in range(2):
                        for d in range(KD):
                            n = b * 4 + hf * 2 + d + 1
                            pool.wait_ge(prh_rdy, n)
                            q = slice(hf * CH, (hf + 1) * CH)
                            pool.tensor_tensor(prl[:, d, q], pf[:, d, :], prh[:, d, q].bitcast(F32), ALU.subtract).then_inc(prl_rdy, 1)

            row_std(1, 0, TB)
            pool.wait_ge(tgb_rdy, 1)
            body(0, True, False)
            row_std(2, TB, B * TB)
            with pool.Fori(1, B) as b:
                body(b, True, True)
            f = B - 1
            pool.wait_ge(wmax_a, 1)
            pool.partition_all_reduce(c_sa, c_sm, P, RMAX).then_inc(wall_rdy, 1)
            pool.wait_ge(wscale_a, 1)

            def weight_q(m):
                wm = wr[:, m, :].rearrange("p (n k) -> p n k", k=QB)
                pool.tensor_tensor(wm, wm, wri[:, m, :].unsqueeze(2).broadcast_to([P, NB, QB]), ALU.mult).then_inc(wq_rdy, 1)

            for s in range(NP):
                if s < 3:
                    weight_q(s)
                pool.wait_ge(vp2_done, f * NP + s + 1)
                pool.wait_ge(y_rdy, f * NP + s)
                pool.tensor_tensor(rstd2, vp2, mhalf[:, 0:2], ALU.pow).then_inc(rstd2_rdy, 1)
            for n in range(5):
                pool.wait_ge(loc_rdy, n + 1)
                pool.partition_all_reduce(c_all[:, n:n + 1], c_loc[:, n:n + 1], P, RMAX).then_inc(all_rdy, 1)

        @block.tensor
        def _(pe):
            def three(dst, pairs, first=True, last=True):
                n = 3 * len(pairs)
                i = 0
                for sh, sl, mh, ml in pairs:
                    for st_, mo in ((sh, mh), (sl, mh), (sh, ml)):
                        mm = pe.matmul(dst, st_, mo, start=first and i == 0, stop=last and i == n - 1)
                        i += 1
                return mm

            def context(b):
                pe.wait_ge(cx_in, 16 * b + 16)
                ge(pe, hc_rdy, b)
                for k in range(2):
                    for d in range(KD):
                        tr = pe.transpose(sb_bank[:, d * J + k * JP:d * J + (k + 1) * JP],
                                          cx[0:JP, k, d * P:(d + 1) * P], ident[0:JP, 0:JP])
                tr.then_inc(cxT_ps, 1)
                pe.wait_ge(cxT_rdy, b + 1)
                for d in range(KD):
                    mm = pe.matmul(sb_bank[:, 2 * J:3 * J], w2b[:, d, :], cxT[:, d, :], start=(d == 0), stop=(d == KD - 1))
                mm.then_inc(cbi_ps, 1)

            def turn_h(b, s):
                pe.wait_ge(h_rdy, b * NP + s + 1)
                ge(pe, hth_rdy, b * NP + s)
                for d in range(KD):
                    for t in range(2):
                        tr = pe.transpose(tb_bank[:, d * PT + t * P:d * PT + (t + 1) * P],
                                          h[:, 2 * s + t, d * P:(d + 1) * P], ident[:])
                tr.then_inc(hT_ps, 1)

            def project(f, s):
                pe.wait_ge(hql_rdy, f * 4 + (s // 2) * 2 + 2)
                pe.wait_ge(prl_rdy, f * 4 + (s // 2) * 2 + 2)
                pe.wait_ge(we_rdy, f + 1)
                ge(pe, x1_rdy, f * NP + max(s - 1, 0))
                for t in range(2):
                    q = slice(s * PT + t * P, s * PT + (t + 1) * P)
                    parts = [(hqh[:, d, q], hql[:, d, q], wmh[:, d, :], wml[:, d, :]) for d in range(KD)]
                    parts += [(prh[:, d, q], prl[:, d, q], wmh[:, KD + d, :], wml[:, KD + d, :]) for d in range(KD)]
                    parts += [(hth[:, d, q], htl[:, d, q], weh[:, d, :], wel[:, d, :]) for d in range(KD)]
                    mm = three(f_bank[s % 2][:, t * D:(t + 1) * D], parts)
                mm.then_inc(f_ps, 1)

            def turn_y(f, s):
                pe.wait_ge(y_rdy, f * NP + s + 1)
                ge(pe, yT_rdy, f * NP + s)
                for d in range(KD):
                    for t in range(2):
                        tr = pe.transpose(yb_bank[:, d * PT + t * P:d * PT + (t + 1) * P],
                                          yb[:, s % 2, t, d * P:(d + 1) * P], ident[:])
                tr.then_inc(yT_ps, 1)

            def score(b, s):
                pe.wait_ge(htl_rdy, b * NP + s + 1)
                if s == 0:
                    pe.wait_ge(cp_rdy, b + 1)
                    pe.wait_ge(cbi_rdy, b + 1)
                else:
                    pe.wait_ge(sc_rdy, b * NP + s)
                for t in range(2):
                    q = slice(s * PT + t * P, s * PT + (t + 1) * P)
                    mm = three(sb_bank[:, t * J:(t + 1) * J],
                               [(hth[:, d, q], htl[:, d, q], cph[:, d, :], cpl[:, d, :]) for d in range(KD)])
                mm.then_inc(sc_ps, 1)

            def turn_a(b, s):
                pe.wait_ge(a_rdy, b * NP + s + 1)
                ge(pe, at_rdy, b * NP + s)
                for k in range(2):
                    for t in range(2):
                        tr = pe.transpose(ab_bank[0:JP, k * PT + t * P:k * PT + (t + 1) * P],
                                          sc[:, s % 2, t, k * JP:(k + 1) * JP], ident[:])
                tr.then_inc(at_ps, 1)

            def attend(b, hf):
                pe.wait_ge(at_rdy, b * NP + 2 * hf + 2)
                pe.wait_ge(cx_rdy, b + 1)
                for d in range(KD):
                    ge(pe, pf_rdy, b * 4 + hf * 2 - 1 + d)
                    mm = three(hq_bank[d], [(cxh[0:JP, k, d * P:(d + 1) * P], cxl[0:JP, k, d * P:(d + 1) * P],
                                             ath[0:JP, k, :], atl[0:JP, k, :]) for k in range(2)])
                    mm.then_inc(hq_ps, 1)

            def batch_max(b):
                pe.wait_ge(diag_rdy, b + 1)
                pe.wait_ge(sc_rdy, b * NP + NP)
                pe.matmul(sb_bank[:, 0:P], ones[:], diag[:], start=True, stop=True).then_inc(m_ps, 1)

            def batch_sum(b):
                pe.wait_ge(eb_rdy, b + 1)
                for d in range(KD):
                    for t in range(TB):
                        pe.matmul(sb_bank[:, P + d:P + d + 1], h[:, t, d * P:(d + 1) * P], eb[:, t:t + 1],
                                  start=(t == 0), stop=(t == TB - 1))
                pe.matmul(sb_bank[:, P + KD:P + KD + 1], ones[:], c_es, start=True, stop=True).then_inc(hc_ps, 1)

            def body(b, scores, proj):
                f = b - 1
                if scores:
                    context(b)
                for s in range(NP):
                    if scores:
                        turn_h(b, s)
                    if proj:
                        project(f, s)
                    if scores and s >= 1:
                        score(b, s - 1)
                    if scores and s >= 2:
                        turn_a(b, s - 2)
                    if proj and s >= 1:
                        turn_y(f, s - 1)
                if scores:
                    score(b, NP - 1)
                if proj:
                    turn_y(f, NP - 1)
                if scores:
                    attend(b, 0)
                    turn_a(b, 2)
                    batch_max(b)
                    turn_a(b, 3)
                    batch_sum(b)
                    attend(b, 1)

            pe.wait_ge(ident_rdy, 1)
            pe.wait_ge(ones_rdy, 1)
            pe.wait_ge(small_in, 16 * 5)
            pe.matmul(f_bank[0][:, 0:D + 3], ones[0:1, :], row[0:1, :], start=True, stop=True).then_inc(rows_ps, 1)
            pe.wait_ge(w2b_rdy, KD)
            body(0, True, False)
            with pe.Fori(1, B) as b:
                body(b, True, True)
            f = B - 1

            def turn_w(m):
                pe.wait_ge(wn_rdy, m + 1)
                for q in range(3):
                    ge(pe, wt_rdy, 3 * m + q - 2)
                    for i in range(2):
                        for k in range(2):
                            at = (2 * q + i) * D + k * P if m < 2 else k * FF + (2 * q + i) * P
                            to = k * D + i * P if m < 2 else i * D + k * P
                            tr = pe.transpose(w_bank[q][:, to:to + P], wr[:, m, at:at + P], ident[:])
                    tr.then_inc(wt_ps, 1)

            for s in range(NP):
                project(f, s)
                if s >= 1:
                    turn_y(f, s - 1)
            turn_y(f, NP - 1)
            for m in range(3):
                turn_w(m)

            def hidden(wh, wl, done, passed):
                with pe.Fori(0, KF) as k:
                    for hf in range(2):
                        pe.wait_ge(half_free[hf], k + 1 + done)
                        for q in range(4):
                            c = 4 * hf + q
                            if passed == 0:
                                pe.wait_ge(xq_rdy, c + 1)
                            n = slice(c * CH, (c + 1) * CH)
                            mm = three(ps[hf][:, q, :],
                                       [(wh[:, d, ds(k * P, P)], wl[:, d, ds(k * P, P)], xh[:, d, n], xl[:, d, n])
                                        for d in range(KD)])
                        mm.then_inc(unit_ps, 1)

            pe.wait_ge(wt_rdy, 9)
            hidden(wgh, wgl, 0, 0)
            hidden(wuh, wul, KF, 1)
            hidden(wuh, wul, 2 * KF, 2)

            def down(c, par):
                pe.wait_ge(os_rdy, c + 1)
                ge(pe, fin_rdy, c - 1)
                for t in range(4):
                    q = slice(t * P, (t + 1) * P)
                    mm = three(ps[par][:, t // 2, (t % 2) * D:(t % 2 + 1) * D],
                               [(oh[:, par, k, q], ol[:, par, k, q], wdh[:, k, :], wdl[:, k, :]) for k in range(KF)])
                mm.then_inc(dn_ps, 1)

            pe.wait_ge(half_free[0], 3 * KF + 1)
            pe.wait_ge(half_free[1], 3 * KF + 1)
            for par in range(2):
                down(par, par)
            with pe.Fori(1, NC // 2) as c2:
                for par in range(2):
                    down(c2 * 2 + par, par)

        @block.scalar
        def _(act):
            act.dma_start(row[0:1, 0:D], b_qv.rearrange("(a n) -> a n", a=1)).then_inc(small_in, 16)
            for n, s in enumerate((g_xattn, g_ffn, b_sim)):
                act.dma_start(row[0:1, D + n:D + n + 1], s.rearrange("(a n) -> a n", a=1)).then_inc(small_in, 16)
            act.dma_start(wcol[:], wsim_v, allow_slow_non_contiguous=True).then_inc(small_in, 16)
            act.preload_act_table(ACT.Exp)
            act.wait_ge(rows_ps, 1)
            act.activation(c_t2, f_bank[0][:, D:D + 2], ACT.Tanh).then_inc(tanh_rdy, 1)
            act.wait_ge(wqv_in, 48)
            act.activation(wmh[:], wmid[:], ACT.Copy).then_inc(wmh_rdy, 1)

            def turned_h(b, s, proj):
                q = slice(s * PT, (s + 1) * PT)
                act.wait_ge(hT_ps, b * NP + s + 1)
                ge(act, pf_rdy, 4 * b)
                act.activation(hTf[:, :, q], tb_bank.rearrange("p (d n) -> p d n", d=KD), ACT.Copy).then_inc(hTf_rdy, 1)
                if proj:
                    act.wait_ge(f_ps, b * NP - NP + s + 1)
                act.activation(hth[:, :, q], tb_bank.rearrange("p (d n) -> p d n", d=KD), ACT.Copy).then_inc(hth_rdy, 1)

            def turned_y(f, s):
                act.wait_ge(yT_ps, f * NP + s + 1)
                act.activation(yT[:, :, ds(f * S + s * PT, PT)], yb_bank.rearrange("p (d n) -> p d n", d=KD),
                               ACT.Copy).then_inc(yT_rdy, 1)

            def exps(b, s):
                act.wait_ge(nm_rdy, b * NP + s + 1)
                for t in range(2):
                    c = 2 * s + t
                    a_ = act.activation(sc[:, s % 2, t, :], sc[:, s % 2, t, :], ACT.Exp, bias=nm[:, c:c + 1],
                                        accum_out=rs[:, c:c + 1])
                a_.then_inc(exp_rdy, 1)

            def turned_a(b, s):
                act.wait_ge(at_ps, b * NP + s + 1)
                ge(act, hq_ps, 4 * b + (s // 2) * 2)
                act.activation(ath[0:JP, :, (s % 2) * PT:(s % 2 + 1) * PT],
                               ab_bank[0:JP, :].rearrange("p (k n) -> p k n", k=2), ACT.Copy).then_inc(ath_rdy, 1)

            def attended(b, hf, proj):
                q = slice(hf * CH, (hf + 1) * CH)
                if proj:
                    act.wait_ge(f_ps, b * NP - NP + 2 * hf + 2)
                for d in range(KD):
                    act.wait_ge(hq_ps, 4 * b + 2 * hf + d + 1)
                    act.activation(hqh[:, d, q], hq_bank[d], ACT.Copy).then_inc(hqh_rdy, 1)

            def product(b, hf):
                q = slice(hf * CH, (hf + 1) * CH)
                for d in range(KD):
                    act.wait_ge(pf_rdy, 4 * b + 2 * hf + d + 1)
                    act.activation(prh[:, d, q], pf[:, d, :], ACT.Copy).then_inc(prh_rdy, 1)

            def body(b, scores, proj):
                f = b - 1
                if scores:
                    act.wait_ge(cxT_ps, b + 1)
                    ge(act, cbi_ps, b)
                    ge(act, cpf_rdy, b)
                    act.activation(cxT[:], sb_bank[:, 0:2 * J].rearrange("p (d j) -> p d j", d=KD), ACT.Copy).then_inc(cxT_rdy, 1)
                    ge(act, hq_ps, 4 * b)
                    act.wait_ge(cx_in, 16 * b + 16)
                    act.activation(cxh[:], cx[:], ACT.Copy).then_inc(cxh_rdy, 1)
                    act.wait_ge(cpf_rdy, b + 1)
                    ge(act, sc_ps, NP * b)
                    act.activation(cph[:], cpf[:], ACT.Copy).then_inc(cph_rdy, 1)
                for s in range(NP):
                    if scores:
                        turned_h(b, s, proj)
                    if scores and s >= 1:
                        exps(b, s - 1)
                    if scores and s >= 2:
                        turned_a(b, s - 2)
                    if proj and s >= 1:
                        turned_y(f, s - 1)
                if scores:
                    exps(b, NP - 1)
                if proj:
                    turned_y(f, NP - 1)
                if scores:
                    attended(b, 0, proj)
                    turned_a(b, 2)
                    act.wait_ge(ngm_rdy, b + 1)
                    act.activation(eb, rm, ACT.Exp, bias=c_ngm, accum_out=c_es).then_inc(eb_rdy, 1)
                    product(b, 0)
                    turned_a(b, 3)
                    act.wait_ge(wef_rdy, b + 1)
                    if proj:
                        act.wait_ge(f_ps, b * NP)
                    act.activation(weh[:], wef[:], ACT.Copy).then_inc(weh_rdy, 1)
                    attended(b, 1, proj)
                    product(b, 1)

            body(0, True, False)
            with act.Fori(1, B) as b:
                body(b, True, True)
            f = B - 1

            def turned_w(m):
                for q in range(3):
                    act.wait_ge(wt_ps, 3 * m + q + 1)
                    act.activation(w_part(m, q, 0), w_seen(m, q), ACT.Copy).then_inc(wth_rdy, 1)

            for s in range(NP):
                if s >= 1:
                    turned_y(f, s - 1)
            turned_y(f, NP - 1)
            for m in range(3):
                turned_w(m)

            act.wait_ge(scales, 1)
            for c in range(NC):
                ge(act, xq_rdy, c - 1)
                act.activation(xqi[:, c % 2], yT[:, :, c * CH:(c + 1) * CH], ACT.Copy, scale=c_ix).then_inc(xqi_rdy, 1)
            act.wait_ge(x1_out, 16 * B)
            with act.Fori(0, KF) as k:
                for hf in range(2):
                    act.wait_ge(unit_ps, k * 2 + hf + 1)
                    act.activation(unit(hid, k, hf), ps_half(hf), ACT.Copy).then_inc(half_free[hf], 1)
            act.preload_act_table(ACT.Sigmoid)
            act.wait_ge(scales, 2)

            def gate_steps(k, hf):
                u = k * 2 + hf
                act.activation(unit(gq, k, hf), unit(hid, k, hf), ACT.Copy, scale=c_cg).then_inc(gq_rdy, 1)
                ge(act, p_rdy, u - 1)
                plain(act)
                act.activation(ag[:, hf, :], unit(hid, k, hf), ACT.Abs, scale=c_cg).then_inc(ag_rdy, 1)
                act.wait_ge(gq_rdy, u + 1)
                act.wait_ge(ag_rdy, u + 1)
                plain(act)
                act.activation(unit(hid, k, hf), unit(gq, k, hf), ACT.Sigmoid, scale=c_sg).then_inc(sig_rdy, 1)

            def up_steps(k, hf):
                u = k * 2 + hf
                act.wait_ge(unit_ps, 2 * NU + u + 1)
                ge(act, o_rdy, u - 1)
                plain(act)
                act.activation(au[:, hf, :], ps_half(hf), ACT.Abs, scale=c_cu).then_inc(au_rdy, 1)
                act.activation(pq[hf][:], unit(hid, k, hf), ACT.Copy, scale=c_cp).then_inc(pq_rdy, 1)

            def halves(steps):
                for hf in range(2):
                    steps(0, hf)
                with act.Fori(1, KF) as k:
                    for hf in range(2):
                        steps(k, hf)

            halves(gate_steps)
            act.wait_ge(scales, 4)
            halves(up_steps)
            act.wait_ge(scales, 5)

            def product_q(c, par):
                ge(act, os_rdy, c - 1)
                act.activation(oq[:, par], hid[:, :, ds(c * CH, CH)], ACT.Copy, scale=c_co).then_inc(oqa_rdy, 1)

            for par in range(2):
                product_q(par, par)
            with act.Fori(1, NC // 2) as c2:
                for par in range(2):
                    product_q(c2 * 2 + par, par)

        @block.vector
        def _(dve):
            done = [0]

            def link(ins):
                done[0] += 1
                ins.then_inc(chain, 1)
                dve.wait_ge(chain, done[0])

            def stats(n, tiles):
                ge(dve, agg_done, n)
                ge(dve, mv_done, n)
                plain(dve)
                for t in range(TB):
                    i_ = dve.bn_stats(st[:, t, :], xa[:, ds(tiles + t, 1), :].rearrange("p a d -> p (a d)"))
                i_.then_inc(bn_done, 1)
                dve.wait_ge(bn_done, n + 1)
                plain(dve)
                for t in range(TB):
                    i_ = dve.bn_aggr(mvb[:, t, :], st[:, t, :])
                i_.then_inc(agg_done, 1)
                dve.wait_ge(agg_done, n + 1)
                dve.tensor_copy(mv[:, ds(tiles, TB), :], mvb).then_inc(mv_done, 1)

            def norm_x(b, s):
                for t in range(2):
                    g = b * TB + 2 * s + t
                    i_ = dve.tensor_scalar(h[:, 2 * s + t, :], xa[:, ds(g, 1), :].rearrange("p a d -> p (a d)"),
                                           mv[:, ds(g, 1), 0:1].rearrange("p a d -> p (a d)"), rstd[:, ds(g, 1)],
                                           ALU.subtract, ALU.mult)
                i_.then_inc(h_rdy, 1)

            def context(b):
                dve.wait_ge(cxT_rdy, b + 1)
                for d in range(KD):
                    i_ = dve.tensor_scalar(cpf[:, d, :], cxT[:, d, :], wcol[:, 2 * KD + d:2 * KD + d + 1],
                                           wcol[:, d:d + 1], ALU.mult, ALU.add)
                i_.then_inc(cpf_rdy, 1)
                dve.wait_ge(cxh_rdy, b + 1)
                dve.tensor_tensor(cxl[:], cx[:], cxh[:].bitcast(F32), ALU.subtract).then_inc(cx_rdy, 1)
                dve.wait_ge(cbi_ps, b + 1)
                dve.tensor_scalar(cbi[:], sb_bank[:, 2 * J:3 * J], c_bs, None, ALU.add).then_inc(cbi_rdy, 1)
                dve.wait_ge(cph_rdy, b + 1)
                dve.tensor_tensor(cpl[:], cpf[:], cph[:].bitcast(F32), ALU.subtract).then_inc(cp_rdy, 1)

            def scored(b, s):
                n = b * NP + s
                dve.wait_ge(sc_ps, n + 1)
                dve.wait_ge(cbi_rdy, b + 1)
                ge(dve, at_ps, n - 1)
                plain(dve)
                for t in range(2):
                    i_ = dve.tensor_tensor_reduce(sc[:, s % 2, t, :], sb_bank[:, t * J:(t + 1) * J], cbi[:], 1.0,
                                                  -3.4e38, ALU.add, ALU.max, rm[:, 2 * s + t:2 * s + t + 1])
                i_.then_inc(sc_rdy, 1)
                dve.wait_ge(sc_rdy, n + 1)
                dve.tensor_scalar(nm[:, 2 * s:2 * s + 2], rm[:, 2 * s:2 * s + 2], -1.0, None, ALU.mult).then_inc(nm_rdy, 1)

            def normed(b, s):
                n = b * NP + s
                dve.wait_ge(exp_rdy, n + 1)
                dve.reciprocal(ri[:, 2 * s:2 * s + 2], rs[:, 2 * s:2 * s + 2]).then_inc(ri_rdy, 1)
                dve.wait_ge(ri_rdy, n + 1)
                for t in range(2):
                    i_ = dve.tensor_scalar(sc[:, s % 2, t, :], sc[:, s % 2, t, :], ri[:, 2 * s + t:2 * s + t + 1],
                                           None, ALU.mult)
                i_.then_inc(a_rdy, 1)

            def turned_a(b, s):
                dve.wait_ge(ath_rdy, b * NP + s + 1)
                q = slice((s % 2) * PT, (s % 2 + 1) * PT)
                dve.tensor_tensor(atl[0:JP, :, q], ab_bank[0:JP, :].rearrange("p (k n) -> p k n", k=2),
                                  ath[0:JP, :, q].bitcast(F32), ALU.subtract).then_inc(at_rdy, 1)

            def attended(b, hf):
                q = slice(hf * CH, (hf + 1) * CH)
                for d in range(KD):
                    n = b * 4 + hf * 2 + d
                    dve.wait_ge(hqh_rdy, n + 1)
                    dve.tensor_tensor(hql[:, d, q], hq_bank[d], hqh[:, d, q].bitcast(F32), ALU.subtract).then_inc(hql_rdy, 1)
                    ge(dve, prl_rdy, n - 1)
                    dve.tensor_tensor(pf[:, d, :], hq_bank[d], hTf[:, d, q], ALU.mult).then_inc(pf_rdy, 1)

            def residual(f, s):
                n = f * NP + s
                g = f * TB + 2 * s
                dve.wait_ge(f_ps, n + 1)
                dve.wait_ge(xb_rdy, n + 1)
                x_ = xa[:, ds(g, 2), :]
                dve.scalar_tensor_tensor(x_, f_bank[s % 2].rearrange("p (t d) -> p t d", t=2), c_tx, x_,
                                         ALU.mult, ALU.add).then_inc(x1_rdy, 1)
                dve.wait_ge(x1_rdy, n + 1)
                plain(dve)
                for t in range(2):
                    i_ = dve.bn_stats(st[:, t, :], xa[:, ds(g + t, 1), :].rearrange("p a d -> p (a d)"))
                i_.then_inc(bn2_done, 1)
                dve.wait_ge(bn2_done, n + 1)
                plain(dve)
                for t in range(2):
                    i_ = dve.bn_aggr(mv2[:, t, :], st[:, t, :])
                i_.then_inc(mv2_done, 1)
                dve.wait_ge(mv2_done, n + 1)
                dve.tensor_scalar(vp2, mv2[:, :, 1], LN_EPS, None, ALU.add).then_inc(vp2_done, 1)

            def norm_x1(f, s):
                n = f * NP + s
                dve.wait_ge(rstd2_rdy, n + 1)
                ge(dve, yT_ps, f * NP + max(s - 1, 0))
                for t in range(2):
                    i_ = dve.tensor_scalar(yb[:, s % 2, t, :], xa[:, ds(f * TB + 2 * s + t, 1), :].rearrange("p a d -> p (a d)"),
                                           mv2[:, t, 0:1], rstd2[:, t:t + 1], ALU.subtract, ALU.mult)
                i_.then_inc(y_rdy, 1)
                dve.wait_ge(y_rdy, n + 1)
                dve.tensor_reduce(ymx[:, ds(n, 1)], yb[:, s % 2].rearrange("p t d -> p (t d)"), AX.X, ALU.max,
                                  apply_absolute_value=True).then_inc(ym_done, 1)

            def body(b, scores, proj):
                f = b - 1
                if scores:
                    ge(dve, hc_ps, b)
                    norm_x(b, 0)
                    norm_x(b, 1)
                    context(b)
                    norm_x(b, 2)
                    norm_x(b, 3)
                for s in range(NP):
                    if proj:
                        residual(f, s)
                    if scores and s >= 1:
                        scored(b, s - 1)
                    if proj:
                        norm_x1(f, s)
                    if scores and s >= 1:
                        normed(b, s - 1)
                    if scores and s >= 2:
                        turned_a(b, s - 2)
                if scores:
                    scored(b, NP - 1)
                    dve.tensor_reduce(c_m1, rm, AX.X, ALU.max).then_inc(m1_rdy, 1)
                    dve.wait_ge(m1_rdy, b + 1)
                    dve.tensor_scalar(diag[:], ident[:], c_m1, None, ALU.mult).then_inc(diag_rdy, 1)
                    normed(b, NP - 1)
                    attended(b, 0)
                    turned_a(b, 2)
                    dve.wait_ge(m_ps, b + 1)
                    dve.tensor_reduce(c_ngm, sb_bank[:, 0:P], AX.X, ALU.max, negate=True).then_inc(ngm_rdy, 1)
                    turned_a(b, 3)
                    dve.wait_ge(hc_ps, b + 1)
                    dve.reciprocal(c_rs, sb_bank[:, P + KD:P + KD + 1]).then_inc(crs_rdy, 1)
                    dve.wait_ge(crs_rdy, b + 1)
                    dve.tensor_scalar(c_hc, sb_bank[:, P:P + KD], c_rs, None, ALU.mult).then_inc(hc_rdy, 1)
                    dve.wait_ge(hc_rdy, b + 1)
                    for d in range(KD):
                        i_ = dve.scalar_tensor_tensor(wef[:, d, :], w3[:, d, :], c_hc[:, d:d + 1], w0[:, d, :], ALU.mult, ALU.add)
                    i_.then_inc(wef_rdy, 1)
                    attended(b, 1)
                    dve.wait_ge(weh_rdy, b + 1)
                    dve.tensor_tensor(wel[:], wef[:], weh[:].bitcast(F32), ALU.subtract).then_inc(we_rdy, 1)

            dve.wait_ge(ones_rdy, 1)
            dve.wait_ge(small_in, 80)
            for d in range(KD):
                dve.tensor_scalar(w2b[:, d, :], ones[:], wcol[:, KD + d:KD + d + 1], None, ALU.mult).then_inc(w2b_rdy, 1)
            dve.wait_ge(x0_in, 16 * NP)
            stats(0, 0)
            dve.wait_ge(mv_done, 1)
            dve.tensor_scalar(rstd[:, 0:TB], mv[:, 0:TB, 1], LN_EPS, None, ALU.add).then_inc(vp_done, 1)
            dve.wait_ge(tanh_rdy, 1)
            link(dve.tensor_copy(c_bs, f_bank[0][:, D + 2:D + 3]))
            dve.tensor_scalar(tgb[:], f_bank[0][:, 0:D], c_tx, None, ALU.mult).then_inc(tgb_rdy, 1)
            dve.wait_ge(wmh_rdy, 1)
            dve.tensor_tensor(wml[:], wmid[:], wmh[:].bitcast(F32), ALU.subtract).then_inc(wml_rdy, 1)
            dve.wait_ge(wml_rdy, 1)
            dve.wait_ge(ident_rdy, 1)
            dve.wait_ge(rstd_rdy, 1)
            body(0, True, False)
            dve.wait_ge(xr_in, 16 * (B - 1))
            with dve.Fori(1, B) as b:
                stats(b, b * TB)
            dve.wait_ge(mv_done, B)
            dve.tensor_scalar(rstd[:, TB:B * TB], mv[:, TB:B * TB, 1], LN_EPS, None, ALU.add).then_inc(vp_done, 1)
            dve.wait_ge(rstd_rdy, 2)
            with dve.Fori(1, B) as b:
                body(b, True, True)

            f = B - 1
            dve.wait_ge(wffn_in, 48)
            link(dve.tensor_reduce(wsc[:].rearrange("p m n -> p (m n)"), wr[:].rearrange("p m (n k) -> p (m n) k", k=QB),
                                   AX.X, ALU.max, apply_absolute_value=True))
            link(dve.tensor_scalar(wsc[:], wsc[:], 1.0 / 7.0, EPS, ALU.mult, ALU.max))
            dve.tensor_reduce(c_sm, wsc[:], AX.X, ALU.max).then_inc(wmax_a, 1)
            dve.reciprocal(wri[:], wsc[:]).then_inc(wscale_a, 1)
            residual(f, 0)
            dve.wait_ge(wall_rdy, 1)
            link(dve.tensor_scalar(c_pw.bitcast(I32), c_sa.bitcast(I32), 0x7F800000, None, ALU.bitwise_and))
            link(dve.reciprocal(c_wt, c_pw))
            dve.tensor_scalar(c_dn, c_pw, 1.0 / W_SCALE, None, ALU.mult)
            dve.wait_ge(wscale_a, 1)
            for m in range(3):
                i_ = dve.tensor_scalar(wsc[:, m, :], wsc[:, m, :], c_wt[:, m:m + 1], W_SCALE, ALU.mult, ALU.mult)
            i_.then_inc(wscale_a, 1)
            for s in range(NP):
                if s >= 1:
                    residual(f, s)
                if s < 3:
                    dve.wait_ge(wq_rdy, s + 1)
                    ge(dve, wn_rdy, s)
                    dve.tensor_scalar(wqi[:], wr[:, s, :], 7.0, -8.0, ALU.min, ALU.max).then_inc(wqi_rdy, 1)
                norm_x1(f, s)
                if s < 3:
                    dve.wait_ge(wqi_rdy, s + 1)
                    if s == 0:
                        dve.wait_ge(wscale_a, 2)
                    dve.tensor_tensor(wr[:, s, :].rearrange("p (n k) -> p n k", k=QB),
                                      wqi[:].rearrange("p (n k) -> p n k", k=QB),
                                      wsc[:, s, :].unsqueeze(2).broadcast_to([P, NB, QB]), ALU.mult).then_inc(wn_rdy, 1)

            def largest(n, counts, m):
                dve.wait_ge(*counts)
                dve.tensor_reduce(c_loc[:, n:n + 1], m, AX.X, ALU.max).then_inc(loc_rdy, 1)

            def overall(n):
                dve.wait_ge(all_rdy, n + 1)
                return c_all[:, n:n + 1]

            largest(0, (ym_done, B * NP), ymx)
            v = overall(0)
            link(dve.tensor_scalar(c_sx, v, 1.0 / QMAX, EPS, ALU.mult, ALU.max))
            dve.reciprocal(c_ix, c_sx).then_inc(scales, 1)
            for m in range(3):
                for q in range(3):
                    dve.wait_ge(wth_rdy, 3 * m + q + 1)
                    part = w_part(m, q, 0)
                    dve.tensor_tensor(w_part(m, q, 1), w_seen(m, q), part, ALU.subtract).then_inc(wt_rdy, 1)
            dve.wait_ge(yT_rdy, B * NP)
            dve.tensor_scalar(c_kg, c_sx, c_dn[:, 0:1], None, ALU.mult).then_inc(half_free[0], 1)
            dve.tensor_scalar(c_ku, c_sx, c_dn[:, 1:2], None, ALU.mult).then_inc(half_free[1], 1)
            dve.wait_ge(half_free[0], 1)
            dve.wait_ge(half_free[1], 1)
            dve.tensor_scalar(c_kgq, c_kg, 1.0 / QMAX, None, ALU.mult)
            dve.tensor_scalar(c_kuq, c_ku, 1.0 / QMAX, None, ALU.mult)
            link(dve.tensor_scalar(c_ft, c_tf, c_dn[:, 2:3], None, ALU.mult))
            for c in range(NC):
                dve.wait_ge(xqi_rdy, c + 1)
                n = slice(c * CH, (c + 1) * CH)
                dve.tensor_copy(xh[:, :, n], xqi[:, c % 2]).then_inc(xh_rdy, 1)
                dve.wait_ge(xh_rdy, c + 1)
                dve.tensor_tensor(xl[:, :, n], xqi[:, c % 2], xh[:, :, n], ALU.subtract).then_inc(xq_rdy, 1)
            with dve.Fori(0, KF) as k:
                for hf in range(2):
                    dve.wait_ge(half_free[hf], k + 2)
                    dve.tensor_reduce(gmx[:, ds(k * 2 + hf, 1)], unit(hid, k, hf), AX.X, ALU.max,
                                      apply_absolute_value=True).then_inc(gm_done, 1)
            largest(1, (gm_done, NU), gmx)
            v = overall(1)
            link(dve.tensor_scalar(c_sg, v, c_kgq, EPS, ALU.mult, ALU.max))
            link(dve.reciprocal(c_rg, c_sg))
            dve.tensor_scalar(c_cg, c_rg, c_kg, None, ALU.mult).then_inc(scales, 1)
            link(dve.tensor_scalar(c_kp, c_sg, 1.0 / 65536.0, None, ALU.mult))
            link(dve.tensor_scalar(c_kpq, c_kp, 1.0 / QMAX, None, ALU.mult))

            def up_max(u):
                dve.wait_ge(unit_ps, NU + u + 1)
                dve.tensor_reduce(umx[:, u:u + 1], ps_half(u % 2), AX.X, ALU.max,
                                  apply_absolute_value=True).then_inc(half_free[u % 2], 1)

            def gated(u):
                k, hf = u // 2, u % 2
                dve.wait_ge(sig_rdy, u + 1)
                ge(dve, p_rdy, u)
                dve.tensor_scalar(sq[:], hid[:, k, hf * HALF:(hf + 1) * HALF], 65536.0, None, ALU.mult).then_inc(sq_rdy, 1)
                dve.wait_ge(sq_rdy, u + 1)
                dve.wait_ge(ag_rdy, u + 1)
                dve.tensor_tensor_reduce(hid[:, k, hf * HALF:(hf + 1) * HALF], ag[:, hf, :], sq[:], 1.0, 0.0,
                                         ALU.mult, ALU.max, pmx[:, u:u + 1]).then_inc(p_rdy, 1)

            up_max(0)
            for u in range(1, NU):
                up_max(u)
                gated(u - 1)
            dve.wait_ge(half_free[1], 2 * KF + 1)
            largest(2, (half_free[0], 2 * KF + 1), umx)
            gated(NU - 1)
            largest(3, (p_rdy, NU), pmx)
            v = overall(2)
            link(dve.tensor_scalar(c_su, v, c_kuq, EPS, ALU.mult, ALU.max))
            link(dve.reciprocal(c_ru, c_su))
            dve.tensor_scalar(c_cu, c_ru, c_ku, None, ALU.mult).then_inc(scales, 1)
            v = overall(3)
            link(dve.tensor_scalar(c_sp, v, c_kpq, EPS, ALU.mult, ALU.max))
            link(dve.reciprocal(c_rp, c_sp))
            dve.tensor_scalar(c_cp, c_rp, c_kp, None, ALU.mult).then_inc(scales, 1)
            link(dve.tensor_scalar(c_ko, c_su, c_sp, None, ALU.mult))

            for u in range(NU):
                k, hf = u // 2, u % 2
                n = slice(hf * HALF, (hf + 1) * HALF)
                dve.wait_ge(au_rdy, u + 1)
                dve.tensor_tensor(gq[:, k, n].bitcast(BF16), gq[:, k, n], ps_half(hf), ALU.mult).then_inc(half_free[hf], 1)
                dve.wait_ge(pq_rdy, u + 1)
                dve.tensor_tensor_reduce(hid[:, k, n], pq[hf][:], au[:, hf, :], 1.0, 0.0, ALU.mult, ALU.max,
                                         omx[:, u:u + 1]).then_inc(o_rdy, 1)
            largest(4, (o_rdy, NU), omx)
            v = overall(4)
            link(dve.tensor_scalar(c_so, v, c_ko, 1.0 / QMAX, ALU.mult, ALU.mult))
            link(dve.tensor_scalar(c_so, c_so, EPS, None, ALU.max))
            link(dve.reciprocal(c_ro, c_so))
            dve.tensor_scalar(c_co, c_ro, c_ko, None, ALU.mult).then_inc(scales, 1)
            link(dve.tensor_scalar(c_fin, c_so, c_ft, None, ALU.mult))
            for hf in range(2):
                dve.wait_ge(half_free[hf], 3 * KF + 1)

            def signed(c, par):
                sg = gq[:, :, ds(c * CH, CH)].bitcast(BF16)
                dve.tensor_scalar(sg, sg, 1.0, -1.0, ALU.min, ALU.max).then_inc(sgn_rdy, 1)
                dve.wait_ge(oqa_rdy, c + 1)
                dve.wait_ge(sgn_rdy, c + 1)
                dve.tensor_tensor(oq[:, par], oq[:, par], sg, ALU.mult).then_inc(oqs_rdy, 1)
                dve.wait_ge(oqs_rdy, c + 1)
                ge(dve, dn_ps, c - 1)
                dve.tensor_copy(oh[:, par], oq[:, par]).then_inc(oh_rdy, 1)
                dve.wait_ge(oh_rdy, c + 1)
                dve.tensor_tensor(ol[:, par], oq[:, par], oh[:, par], ALU.subtract).then_inc(os_rdy, 1)

            def final(c, c2, par):
                dve.wait_ge(dn_ps, c + 1)
                dve.wait_ge((xo_in, xo_in1)[par], c2 * 16 + 16)
                y_ = xo[:, par].rearrange("p t d -> p (t d)")
                dve.scalar_tensor_tensor(y_, ps[par][:, 0:2, :].rearrange("p a n -> p (a n)"), c_fin, y_,
                                         ALU.mult, ALU.add).then_inc(fin_rdy, 1)

            signed(0, 0)
            signed(1, 1)
            final(0, 0, 0)
            with dve.Fori(1, NC // 2) as c2:
                signed(c2 * 2, 0)
                final(c2 * 2 - 1, c2 - 1, 1)
                signed(c2 * 2 + 1, 1)
                final(c2 * 2, c2, 0)
            final(NC - 1, NC // 2 - 1, 1)


_INS = ["x", "ctx_1024", "g_xattn", "g_ffn", "L0_xattn_w_sim", "L0_xattn_b_sim", "L0_xattn_W_qv", "L0_xattn_b_qv",
        "L0_ffn_w_gate", "L0_ffn_w_up", "L0_ffn_w_down"]


def kernel(**inputs):
    import numpy as _np
    import concourse.bacc as _bacc
    from concourse.bass_utils import run_bass_kernel_spmd as _run

    nc = _bacc.Bacc("TRN2", target_bir_lowering=False, num_devices=1)
    arrays, args = {}, []
    for name in _INS:
        v = _np.ascontiguousarray(inputs[name])
        arrays[f"in_{name}"] = v
        args.append(nc.dram_tensor(f"in_{name}", v.shape, mybir.dt.from_np(v.dtype), kind="ExternalInput").ap())
    out = nc.dram_tensor("out_dram", (B, S, D), F32, kind="ExternalOutput").ap()
    build(nc, *args, out)
    r = _run(nc, [arrays], core_ids=[0])
    return r.results[0]["out_dram"]
```

```python
from contextlib import ExitStack

import concourse.bass as bass
from concourse import mybir
from concourse.alu_op_type import AluOpType as ALU

F32 = mybir.dt.float32
F32R = mybir.dt.float32r
F16 = mybir.dt.float16
BF16 = mybir.dt.bfloat16
I16 = mybir.dt.int16
U16 = mybir.dt.uint16
I32 = mybir.dt.int32
ACT = mybir.ActivationFunctionType
AX = mybir.AxisListType
RMAX = bass.bass_isa.ReduceOp.max
ds = bass.ds

P = 128
B, S, D = 4, 1024, 256
J = 154
JP = J // 2
FF = 768
KD = D // P
KF = FF // P
TOK = B * S
TB = S // P
NP = TB // 2
PT = 2 * P
HALF = TOK // 2
NU = 2 * KF
CH = 512
NC = TOK // CH
CD = 256
ND = TOK // CD
SLOTS = 4
QB = 32
NB = FF * D // P // QB
WE = FF * D // P
QMAX = 32767.0
EPS = 1e-12
LN_EPS = 1e-5
COLS = 320
W_SCALE = 2.0 ** 11


def build(nc, x, ctx, g_xattn, g_ffn, w_sim, b_sim, w_qv, b_qv, w_gate, w_up, w_down, out):
    x1_dram = nc.dram_tensor("x1_scratch", (TOK, D), F32, kind="Internal").ap()

    base = -(-nc.sbuf_base // 64) * 64
    top = [base]

    def region(size):
        at = top[0]
        top[0] += -(-size // 32) * 32
        assert top[0] <= nc.sbuf_usable_end, (top[0], nc.sbuf_usable_end)
        return [at, at + size]

    def place(where, name, shape, dt, size_of={F32: 4, F32R: 4, I32: 4, F16: 2, BF16: 2, I16: 2, U16: 2}):
        n = size_of[dt]
        for k in shape[1:]:
            n *= k
        at = where[0]
        where[0] += -(-n // 32) * 32
        assert where[0] <= where[1], (name, where)
        return nc.alloc_sbuf_tensor_at(name, shape, dt, offset=at)

    r_hid = region(KF * TOK * 4)
    r_sgn = region(KF * TOK * 2)
    r_x = region(2 * KD * TOK * 2)
    r_wg = region(2 * KD * FF * 2)
    r_wu = region(2 * KD * FF * 2)
    r_wd = region(2 * KF * D * 2)
    r_tmp = region(12288)
    r_own = region(512 + 1280)

    def copy_of(r):
        return [r[0], r[1]]

    ident = place(r_own, "ident", [P, P], F32)
    cols = place(r_own, "cols", [P, COLS], F32)
    used = [0]

    def col(n=1):
        used[0] += n
        assert used[0] <= COLS
        return cols[:, used[0] - n:used[0]]

    hid = place(copy_of(r_hid), "hid", [P, KF, TOK], F32)
    gq = place(copy_of(r_sgn), "gq", [P, KF, TOK], I16)
    a = copy_of(r_x)
    xh = place(a, "xh", [P, KD, TOK], F16)
    xl = place(a, "xl", [P, KD, TOK], F16)
    a = copy_of(r_wg)
    wgh = place(a, "wgh", [P, KD, FF], F16)
    wgl = place(a, "wgl", [P, KD, FF], F16)
    a = copy_of(r_wu)
    wuh = place(a, "wuh", [P, KD, FF], F16)
    wul = place(a, "wul", [P, KD, FF], F16)
    a = copy_of(r_wd)
    wdh = place(a, "wdh", [P, KF, D], F16)
    wdl = place(a, "wdl", [P, KF, D], F16)
    a = copy_of(r_tmp)
    ag = place(a, "ag", [P, 2, HALF], I16)
    sq = place(a, "sq", [P, HALF], U16)
    a = copy_of(r_tmp)
    au = place(a, "au", [P, 2, HALF], I16)
    pq = [place(a, "pq0", [P, HALF], I16), place(copy_of(r_wg), "pq1", [P, HALF], I16)]
    oq = place(copy_of(r_tmp), "oq", [P, 2, KF, CD], I16)
    a = copy_of(r_x)
    oh = place(a, "oh", [P, 2, KF, CD], F16)
    ol = place(a, "ol", [P, 2, KF, CD], F16)
    xo = place([r_wg[0], r_wu[1]], "xo", [P, SLOTS, CD // P, D], F32)

    a = copy_of(r_sgn)
    yT = place(a, "yT", [P, KD, TOK], F32)
    xqi = place(copy_of(a), "xqi", [P, 2, KD, CH], I16)
    hTf = place(a, "hTf", [P, KD, S], F32)
    ath = place(a, "ath", [JP, 2, CH], F32R)
    atl = place(a, "atl", [JP, 2, CH], F32R)
    a = copy_of(r_hid)
    xa = place(a, "xa", [P, B * TB, D], F32)
    hth = place(a, "hth", [P, KD, S], F32R)
    htl = place(a, "htl", [P, KD, S], F32R)
    wmid = place(copy_of(a), "wmid", [P, 2 * KD, D], F32)
    hqh = place(a, "hqh", [P, KD, S], F32R)
    hql = place(a, "hql", [P, KD, S], F32R)
    prh = place(a, "prh", [P, KD, S], F32R)
    prl = place(a, "prl", [P, KD, S], F32R)
    wmh = place(a, "wmh", [P, 2 * KD, D], F32R)
    wml = place(a, "wml", [P, 2 * KD, D], F32R)
    weh = place(a, "weh", [P, KD, D], F32R)
    wel = place(a, "wel", [P, KD, D], F32R)
    w0 = place(a, "w0", [P, KD, D], F32)
    w3 = place(a, "w3", [P, KD, D], F32)
    a = copy_of(r_x)
    wr = place(a, "wr", [P, 3, WE], F32)
    h = place(a, "h", [P, TB, D], F32)
    wqi = place(a, "wqi", [P, WE], I16)
    wsc = place(a, "wsc", [P, NB], F32)
    wri = place(a, "wri", [P, NB], F32)
    a = [r_wg[0], r_wd[1]]
    cx = place(a, "cx", [JP, 2, D], F32)
    cxh = place(a, "cxh", [JP, 2, D], F32R)
    cxl = place(a, "cxl", [JP, 2, D], F32R)
    cxT = place(a, "cxT", [P, KD, J], F32)
    cpf = place(a, "cpf", [P, KD, J], F32)
    cph = place(a, "cph", [P, KD, J], F32R)
    cpl = place(a, "cpl", [P, KD, J], F32R)
    cbi = place(a, "cbi", [P, J], F32)
    wef = place(a, "wef", [P, KD, D], F32)
    w2b = place(a, "w2b", [P, KD, P], F32)
    ones = place(a, "ones", [P, P], F32)
    diag = place(a, "diag", [P, P], F32)
    row = place(a, "row", [1, D + 3], F32)
    hrow = place(a, "hrow", [1, D], F32)
    wcol = place(a, "wcol", [P, 3 * KD], F32)
    a = copy_of(r_tmp)
    yb = place(a, "yb", [P, 2, 2, D], F32)
    sc = place(a, "sc", [P, 2, 2, J], F32)
    pf = place(a, "pf", [P, 2, CH], F32)
    tgb = place(a, "tgb", [P, D], F32)
    st = place(a, "st", [P, TB, 6], F32)

    mv = col(2 * B * TB).rearrange("p (t s) -> p t s", s=2)
    mvb = col(2 * TB).rearrange("p (t s) -> p t s", s=2)
    rstd = col(B * TB)
    mhalf = col(B * TB)
    mv2 = col(4).rearrange("p (t s) -> p t s", s=2)
    vp2, rstd2 = col(2), col(2)
    rm, nm = col(TB), col(TB)
    rs, ri = col(TB), col(TB)
    eb = col(TB)
    ymx = col(B * NP)
    gmx, umx, pmx, omx = col(NU), col(NU), col(NU), col(NU)
    c_m1, c_ngm, c_es, c_rs, c_hc = col(), col(), col(), col(), col(KD)
    c_t2 = col(2)
    c_tx, c_tf = c_t2[:, 0:1], c_t2[:, 1:2]
    c_bs = col()
    c_sm, c_sa, c_pw, c_wt, c_dn = col(), col(), col(), col(), col(3)
    c_loc, c_all = col(5), col(5)
    c_sx, c_ix, c_kg, c_kgq, c_ku, c_kuq = (col() for _ in range(6))
    c_sg, c_rg, c_cg, c_kp, c_kpq = (col() for _ in range(5))
    c_su, c_ru, c_cu, c_sp, c_rp, c_cp = (col() for _ in range(6))
    c_ko, c_so, c_ro, c_co, c_ft, c_fin = (col() for _ in range(6))

    SUM = P + D + 8
    ps = [nc.alloc_psum_tensor(f"ps{i}", [P, 4, 512], F32) for i in range(2)]
    tb_bank, sb_bank, ab_bank, yb_bank = ps[0][:, 0, :], ps[0][:, 1, :], ps[0][:, 2, :], ps[0][:, 3, :]
    hq_bank = [ps[1][:, 0, :], ps[1][:, 1, :]]
    f_bank = [ps[1][:, 2, :], ps[1][:, 3, :]]

    x_v = x.rearrange("b (t p) d -> p (b t) d", p=P)
    ctx_v = ctx.rearrange("b (k p) d -> b p k d", p=JP)
    wqv_v = w_qv.rearrange("(k p) n -> p k n", p=P)
    wsim_v = w_sim.rearrange("(k p) -> p k", p=P)
    x1_v = x1_dram.rearrange("(t p) d -> p t d", p=P)
    out_v = out.rearrange("b (t p) d -> p (b t) d", p=P)

    with ExitStack() as stack:
        def sem(name):
            return stack.enter_context(nc.semaphore(name))

        x0_in, x1_in, x2_in, x3_in, cx_in, small_in, wqv_in, wffn_in = map(sem, ("x0_in", "x1_in", "x2_in", "x3_in", "cx_in", "small_in", "wqv_in", "wffn_in"))
        x1_out = sem("x1_out")
        xo_in = [sem(f"xo_in{i}") for i in range(SLOTS)]
        out_out = [sem(f"out_out{i}") for i in range(SLOTS)]
        const_a, ident_rdy, mhalf_rdy, ones_rdy, rows_ps, tanh_rdy, tgb_rdy, w2b_rdy, wmh_rdy, wml_rdy = map(
            sem, ("const_a", "ident_rdy", "mhalf_rdy", "ones_rdy", "rows_ps", "tanh_rdy", "tgb_rdy", "w2b_rdy", "wmh_rdy", "wml_rdy"))
        bn_done, agg_done, mv_done, vp_done, rstd_rdy, h_rdy, xb_rdy = map(sem, ("bn_done", "agg_done", "mv_done", "vp_done", "rstd_rdy", "h_rdy", "xb_rdy"))
        cxT_ps, cxT_rdy, cbi_ps, cbi_rdy, cpf_rdy, cph_rdy, cp_rdy, cxh_rdy, cx_rdy = map(
            sem, ("cxT_ps", "cxT_rdy", "cbi_ps", "cbi_rdy", "cpf_rdy", "cph_rdy", "cp_rdy", "cxh_rdy", "cx_rdy"))
        hT_ps, hTf_rdy, hth_rdy, htl_rdy = map(sem, ("hT_ps", "hTf_rdy", "hth_rdy", "htl_rdy"))
        sc_ps, sc_rdy, nm_rdy, exp_rdy, ri_rdy, a_rdy = map(sem, ("sc_ps", "sc_rdy", "nm_rdy", "exp_rdy", "ri_rdy", "a_rdy"))
        at_ps, ath_rdy, at_rdy = map(sem, ("at_ps", "ath_rdy", "at_rdy"))
        hq_ps, hqh_rdy, hql_rdy, pf_rdy, prh_rdy, prl_rdy = map(sem, ("hq_ps", "hqh_rdy", "hql_rdy", "pf_rdy", "prh_rdy", "prl_rdy"))
        m1_rdy, diag_rdy, m_ps, ngm_rdy, eb_rdy, hrow_ps, hrow_rdy, hc_ps, crs_rdy, hc_rdy = map(
            sem, ("m1_rdy", "diag_rdy", "m_ps", "ngm_rdy", "eb_rdy", "hrow_ps", "hrow_rdy", "hc_ps", "crs_rdy", "hc_rdy"))
        wef_rdy, weh_rdy, we_rdy = map(sem, ("wef_rdy", "weh_rdy", "we_rdy"))
        f_ps, x1_rdy, bn2_done, mv2_done, vp2_done, rstd2_rdy, y_rdy, ym_done, yT_ps, yT_rdy = map(
            sem, ("f_ps", "x1_rdy", "bn2_done", "mv2_done", "vp2_done", "rstd2_rdy", "y_rdy", "ym_done", "yT_ps", "yT_rdy"))
        wchain, wmax_rdy, wall_rdy, wq_rdy, wn_rdy, wt_ps, wth_rdy, wt_rdy = map(
            sem, ("wchain", "wmax_rdy", "wall_rdy", "wq_rdy", "wn_rdy", "wt_ps", "wth_rdy", "wt_rdy"))
        loc_rdy, all_rdy, chain, scales = map(sem, ("loc_rdy", "all_rdy", "chain", "scales"))
        xqi_rdy, xh_rdy, xq_rdy, unit_ps, gm_done = map(sem, ("xqi_rdy", "xh_rdy", "xq_rdy", "unit_ps", "gm_done"))
        half_free = [sem("half0_free"), sem("half1_free")]
        gq_rdy, ag_rdy, sig_rdy, sq_rdy, p_rdy, pq_rdy, au_rdy, o_rdy = map(
            sem, ("gq_rdy", "ag_rdy", "sig_rdy", "sq_rdy", "p_rdy", "pq_rdy", "au_rdy", "o_rdy"))
        oqa_rdy, sgn_rdy, oqs_rdy, oh_rdy, os_rdy, dn_ps, fin_rdy = map(
            sem, ("oqa_rdy", "sgn_rdy", "oqs_rdy", "oh_rdy", "os_rdy", "dn_ps", "fin_rdy"))

        passed = sem("passed")

        block = stack.enter_context(nc.Block())

        def unit(t, k, hf):
            return t[:, ds(k, 1), hf * HALF:(hf + 1) * HALF].rearrange("p a n -> p (a n)")

        def ps_half(hf):
            return ps[hf][:].rearrange("p a n -> p (a n)")

        w_bank = [tb_bank, sb_bank, ab_bank]

        def w_part(m, q, low):
            if m == 2:
                return (wdh, wdl)[low][:, 2 * q:2 * q + 2, :].rearrange("p k n -> p (k n)")
            return ((wgh, wgl), (wuh, wul))[m][low][:, :, q * D:(q + 1) * D]

        def w_seen(m, q):
            return w_bank[q] if m == 2 else w_bank[q].rearrange("p (k n) -> p k n", k=KD)

        def ge(eng, s, n):
            if not isinstance(n, int) or n > 0:
                eng.wait_ge(s, n)

        def plain(eng):
            eng.sem_inc(passed, 1)

        @block.sync
        def _(sp):
            for t in range(0, TB, 2):
                sp.dma_start(xa[:, t:t + 2, :], x_v[:, t:t + 2, :]).then_inc(x0_in, 16)
            sp.dma_start(cx[:], ctx_v[0]).then_inc(cx_in, 16)
            sp.dma_start(xa[:, TB:2 * TB, :], x_v[:, TB:2 * TB, :]).then_inc(x1_in, 16)
            sp.dma_start(wmid[:], wqv_v[:, KD:3 * KD, :]).then_inc(wqv_in, 16)
            sp.dma_start(w0[:], wqv_v[:, 0:KD, :]).then_inc(wqv_in, 16)
            sp.dma_start(w3[:], wqv_v[:, 3 * KD:4 * KD, :]).then_inc(wqv_in, 16)
            for b, in_ in ((2, x2_in), (3, x3_in)):
                sp.dma_start(xa[:, b * TB:(b + 1) * TB, :], x_v[:, b * TB:(b + 1) * TB, :]).then_inc(in_, 16)
            for m, w in enumerate((w_gate, w_up)):
                sp.dma_start(wr[:, m, :].rearrange("p (k n) -> p k n", n=D),
                             w.rearrange("(k p) n -> p k n", p=P)).then_inc(wffn_in, 16)
            sp.dma_start(wr[:, 2, :].rearrange("p (k n) -> p k n", n=FF),
                         w_down.rearrange("(k p) n -> p k n", p=P)).then_inc(wffn_in, 16)
            with sp.Fori(1, B) as b:
                sp.wait_ge(cxT_ps, b)
                sp.wait_ge(cx_rdy, b)
                sp.dma_start(cx[:], ctx_v[ds(b, 1)].rearrange("b p k d -> p (b k) d")).then_inc(cx_in, 16)
            with sp.Fori(0, B) as b:
                sp.wait_ge(x1_rdy, b * NP + NP)
                sp.dma_start(x1_v[:, ds(b * TB, TB), :], xa[:, ds(b * TB, TB), :]).then_inc(x1_out, 16)
            sp.wait_ge(x1_out, 16 * B)
            sp.wait_ge(unit_ps, 3 * NU)
            sp.wait_ge(o_rdy, NU)
            for i in range(SLOTS):
                sp.dma_start(xo[:, i], x1_v[:, 2 * i:2 * i + 2, :]).then_inc(xo_in[i], 16)

            def store(g, i):
                sp.wait_ge(fin_rdy, g * SLOTS + i + 1)
                sp.dma_start(out_v[:, ds((g * SLOTS + i) * 2, 2), :], xo[:, i]).then_inc(out_out[i], 16)

            with sp.Fori(0, ND // SLOTS - 1) as g:
                for i in range(SLOTS):
                    store(g, i)
                    sp.wait_ge(out_out[i], g * 16 + 16)
                    sp.dma_start(xo[:, i], x1_v[:, ds(((g + 1) * SLOTS + i) * 2, 2), :]).then_inc(xo_in[i], 16)
            for i in range(SLOTS):
                store(ND // SLOTS - 1, i)
            for i in range(SLOTS):
                sp.wait_ge(out_out[i], 16 * (ND // SLOTS))

        @block.gpsimd
        def _(pool):
            pool.memset(ident[:], 0.0).then_inc(const_a, 1)
            pool.memset(mhalf, -0.5).then_inc(mhalf_rdy, 1)
            pool.memset(ones[:], 1.0).then_inc(ones_rdy, 1)
            pool.wait_ge(const_a, 1)
            pool.affine_select(out=ident[:], in_=ident[:], compare_op=ALU.not_equal, fill=1.0, base=0,
                               pattern=[[-1, P]], channel_multiplier=1).then_inc(ident_rdy, 1)

            def row_std(b):
                t = slice(b * TB, (b + 1) * TB)
                pool.wait_ge(vp_done, b + 1)
                pool.tensor_tensor(rstd[:, t], rstd[:, t], mhalf[:, t], ALU.pow).then_inc(rstd_rdy, 1)

            def context_v(b):
                pool.wait_ge(cxh_rdy, b + 1)
                pool.tensor_tensor(cxl[:], cx[:], cxh[:].bitcast(F32), ALU.subtract).then_inc(cx_rdy, 1)

            def context_k(b):
                pool.wait_ge(cph_rdy, b + 1)
                pool.tensor_tensor(cpl[:], cpf[:], cph[:].bitcast(F32), ALU.subtract).then_inc(cp_rdy, 1)

            def product(b, hf):
                for d in range(KD):
                    pool.wait_ge(prh_rdy, b * 4 + hf * 2 + d + 1)
                    q = slice(hf * CH, (hf + 1) * CH)
                    pool.tensor_tensor(prl[:, d, q], pf[:, d, :], prh[:, d, q].bitcast(F32), ALU.subtract).then_inc(prl_rdy, 1)

            def y_std(f, s):
                pool.wait_ge(vp2_done, f * NP + s + 1)
                ge(pool, y_rdy, f * NP + s)
                pool.tensor_tensor(rstd2, vp2, mhalf[:, 0:2], ALU.pow).then_inc(rstd2_rdy, 1)

            def weight_q(m):
                pool.wait_ge(wmax_rdy, m + 1)
                plain(pool)
                pool.partition_all_reduce(c_sa, c_sm, P, RMAX).then_inc(wall_rdy, 1)
                wm = wr[:, ds(m, 1), :].rearrange("p a (n k) -> p (a n) k", k=QB)
                pool.tensor_tensor(wm, wm, wri[:].unsqueeze(2).broadcast_to([P, NB, QB]), ALU.mult).then_inc(wq_rdy, 1)

            def scores(b, proj):
                for s in range(NP):
                    pool.wait_ge(hth_rdy, b * NP + s + 1)
                    q = slice(s * PT, (s + 1) * PT)
                    pool.tensor_tensor(htl[:, :, q], hTf[:, :, q], hth[:, :, q].bitcast(F32), ALU.subtract).then_inc(htl_rdy, 1)
                    if proj:
                        y_std(b - 1, s)
                    elif s < B - 1:
                        row_std(s + 1)
                    pool.wait_ge(h_rdy, b * NP + s + 1)
                    t = ds(b * TB + 2 * s, 2)
                    pool.tensor_tensor(xa[:, t, :], xa[:, t, :], tgb[:].unsqueeze(1).broadcast_to([P, 2, D]), ALU.add).then_inc(xb_rdy, 1)

            pool.wait_ge(mhalf_rdy, 1)
            row_std(0)
            context_v(0)
            context_k(0)
            pool.wait_ge(tgb_rdy, 1)
            scores(0, False)
            with pool.Fori(1, B) as b:
                product(b - 1, 0)
                context_k(b)
                weight_q(b - 1)
                product(b - 1, 1)
                context_v(b)
                scores(b, True)
            product(B - 1, 0)
            product(B - 1, 1)
            for s in range(NP):
                y_std(B - 1, s)
            for n in range(5):
                pool.wait_ge(loc_rdy, n + 1)
                pool.partition_all_reduce(c_all[:, n:n + 1], c_loc[:, n:n + 1], P, RMAX).then_inc(all_rdy, 1)

        @block.tensor
        def _(pe):
            def three(dst, pairs, first=True, last=True):
                n = 3 * len(pairs)
                i = 0
                for sh, sl, mh, ml in pairs:
                    for st_, mo in ((sh, mh), (sl, mh), (sh, ml)):
                        mm = pe.matmul(dst, st_, mo, start=first and i == 0, stop=last and i == n - 1)
                        i += 1
                return mm

            def turn_context(b):
                pe.wait_ge(cx_in, 16 * b + 16)
                ge(pe, hTf_rdy, b * NP)
                for k in range(2):
                    for d in range(KD):
                        tr = pe.transpose(tb_bank[:, d * J + k * JP:d * J + (k + 1) * JP],
                                          cx[0:JP, k, d * P:(d + 1) * P], ident[0:JP, 0:JP])
                tr.then_inc(cxT_ps, 1)

            def context_bias(b):
                pe.wait_ge(cxT_rdy, b + 1)
                for d in range(KD):
                    mm = pe.matmul(tb_bank[:, 2 * J:3 * J], w2b[:, d, :], cxT[:, d, :], start=(d == 0), stop=(d == KD - 1))
                mm.then_inc(cbi_ps, 1)

            def turn_h(b, s):
                pe.wait_ge(h_rdy, b * NP + s + 1)
                if s == 0:
                    pe.wait_ge(cbi_rdy, b + 1)
                else:
                    pe.wait_ge(hTf_rdy, b * NP + s)
                for d in range(KD):
                    for t in range(2):
                        tr = pe.transpose(tb_bank[:, d * PT + t * P:d * PT + (t + 1) * P],
                                          h[:, 2 * s + t, d * P:(d + 1) * P], ident[:])
                tr.then_inc(hT_ps, 1)

            def project(f, s):
                pe.wait_ge(hql_rdy, f * 4 + (s // 2) * 2 + 2)
                pe.wait_ge(prl_rdy, f * 4 + (s // 2) * 2 + 2)
                ge(pe, x1_rdy, f * NP + max(s - 1, 0))
                for t in range(2):
                    q = slice(s * PT + t * P, s * PT + (t + 1) * P)
                    parts = [(hqh[:, d, q], hql[:, d, q], wmh[:, d, :], wml[:, d, :]) for d in range(KD)]
                    parts += [(prh[:, d, q], prl[:, d, q], wmh[:, KD + d, :], wml[:, KD + d, :]) for d in range(KD)]
                    three(f_bank[s % 2][:, t * D:(t + 1) * D], parts, last=False)
                    pe.wait_ge(we_rdy, f + 1)
                    parts = [(hth[:, d, q], htl[:, d, q], weh[:, d, :], wel[:, d, :]) for d in range(KD)]
                    mm = three(f_bank[s % 2][:, t * D:(t + 1) * D], parts, first=False)
                mm.then_inc(f_ps, 1)

            def turn_y(f, s):
                pe.wait_ge(y_rdy, f * NP + s + 1)
                ge(pe, yT_rdy, f * NP + s)
                for d in range(KD):
                    for t in range(2):
                        tr = pe.transpose(yb_bank[:, d * PT + t * P:d * PT + (t + 1) * P],
                                          yb[:, s % 2, t, d * P:(d + 1) * P], ident[:])
                tr.then_inc(yT_ps, 1)

            def score(b, s):
                pe.wait_ge(htl_rdy, b * NP + s + 1)
                if s == 0:
                    pe.wait_ge(cp_rdy, b + 1)
                    ge(pe, hc_rdy, b)
                else:
                    pe.wait_ge(sc_rdy, b * NP + s)
                for t in range(2):
                    q = slice(s * PT + t * P, s * PT + (t + 1) * P)
                    mm = three(sb_bank[:, t * J:(t + 1) * J],
                               [(hth[:, d, q], htl[:, d, q], cph[:, d, :], cpl[:, d, :]) for d in range(KD)])
                mm.then_inc(sc_ps, 1)

            def turn_a(b, s):
                pe.wait_ge(a_rdy, b * NP + s + 1)
                ge(pe, at_rdy, b * NP + s)
                for k in range(2):
                    for t in range(2):
                        tr = pe.transpose(ab_bank[0:JP, k * PT + t * P:k * PT + (t + 1) * P],
                                          sc[:, s % 2, t, k * JP:(k + 1) * JP], ident[:])
                tr.then_inc(at_ps, 1)

            def attend(b, hf, d):
                if d == 0:
                    pe.wait_ge(at_rdy, b * NP + 2 * hf + 2)
                    pe.wait_ge(cx_rdy, b + 1)
                ge(pe, pf_rdy, b * 4 + (hf * 2 - 1 + d if hf else 0))
                mm = three(hq_bank[d], [(cxh[0:JP, k, d * P:(d + 1) * P], cxl[0:JP, k, d * P:(d + 1) * P],
                                         ath[0:JP, k, :], atl[0:JP, k, :]) for k in range(2)])
                mm.then_inc(hq_ps, 1)

            def batch_max(b):
                pe.wait_ge(diag_rdy, b + 1)
                pe.wait_ge(sc_rdy, b * NP + NP)
                pe.matmul(sb_bank[:, 0:P], ones[:], diag[:], start=True, stop=True).then_inc(m_ps, 1)

            def batch_sum(b):
                pe.wait_ge(eb_rdy, b + 1)
                for t in range(TB):
                    pe.matmul(sb_bank[0:1, P:P + D], eb[:, t:t + 1], h[:, t, :], start=(t == 0), stop=(t == TB - 1))
                pe.matmul(sb_bank[:, SUM:SUM + 1], ones[:], c_es, start=True, stop=True).then_inc(hrow_ps, 1)

            def batch_cols(b):
                pe.wait_ge(hrow_rdy, b + 1)
                pe.wait_ge(crs_rdy, b + 1)
                for d in range(KD):
                    mm = pe.matmul(sb_bank[:, SUM + 1 + d:SUM + 2 + d], hrow[0:1, d * P:(d + 1) * P], ones[0:1, 0:1],
                                   start=True, stop=True)
                mm.then_inc(hc_ps, 1)

            def scores(b, proj):
                f = b - 1
                for s in range(NP):
                    turn_h(b, s)
                    if proj:
                        project(f, s)
                    if s >= 1:
                        score(b, s - 1)
                    if s >= 2:
                        turn_a(b, s - 2)
                    if proj and s >= 1:
                        turn_y(f, s - 1)
                score(b, NP - 1)
                attend(b, 0, 0)
                if proj:
                    turn_y(f, NP - 1)

            def summary(b, more):
                batch_max(b)
                attend(b, 0, 1)
                turn_a(b, 2)
                if more:
                    turn_context(b + 1)
                turn_a(b, 3)
                if more:
                    context_bias(b + 1)
                batch_sum(b)
                attend(b, 1, 0)
                batch_cols(b)
                attend(b, 1, 1)

            pe.wait_ge(ident_rdy, 1)
            pe.wait_ge(ones_rdy, 1)
            pe.wait_ge(small_in, 16 * 5)
            pe.matmul(f_bank[0][:, 0:D + 3], ones[0:1, :], row[0:1, :], start=True, stop=True).then_inc(rows_ps, 1)
            pe.wait_ge(w2b_rdy, KD)
            turn_context(0)
            context_bias(0)
            scores(0, False)
            with pe.Fori(1, B) as b:
                summary(b - 1, True)
                scores(b, True)
            summary(B - 1, False)
            f = B - 1

            def turn_w(m):
                pe.wait_ge(wn_rdy, m + 1)
                for q in range(3):
                    ge(pe, wt_rdy, 3 * m + q - 2)
                    for i in range(2):
                        for k in range(2):
                            at = (2 * q + i) * D + k * P if m < 2 else k * FF + (2 * q + i) * P
                            to = k * D + i * P if m < 2 else i * D + k * P
                            tr = pe.transpose(w_bank[q][:, to:to + P], wr[:, m, at:at + P], ident[:])
                    tr.then_inc(wt_ps, 1)

            for s in range(NP):
                project(f, s)
                if s < 3:
                    turn_w(s)
                if s >= 1:
                    turn_y(f, s - 1)
            turn_y(f, NP - 1)

            def hidden(wh, wl, done, passed):
                with pe.Fori(0, KF) as k:
                    for hf in range(2):
                        pe.wait_ge(half_free[hf], k + 1 + done)
                        for q in range(4):
                            c = 4 * hf + q
                            if passed == 0:
                                pe.wait_ge(xq_rdy, c + 1)
                            n = slice(c * CH, (c + 1) * CH)
                            mm = three(ps[hf][:, q, :],
                                       [(wh[:, d, ds(k * P, P)], wl[:, d, ds(k * P, P)], xh[:, d, n], xl[:, d, n])
                                        for d in range(KD)])
                        mm.then_inc(unit_ps, 1)

            pe.wait_ge(wt_rdy, 9)
            hidden(wgh, wgl, 0, 0)
            hidden(wuh, wul, KF, 1)
            hidden(wuh, wul, 2 * KF, 2)

            def down(c, par):
                pe.wait_ge(os_rdy, c + 1)
                ge(pe, fin_rdy, c - 1)
                for t in range(CD // P):
                    q = slice(t * P, (t + 1) * P)
                    mm = three(ps[par][:, 0, t * D:(t + 1) * D],
                               [(oh[:, par, k, q], ol[:, par, k, q], wdh[:, k, :], wdl[:, k, :]) for k in range(KF)])
                mm.then_inc(dn_ps, 1)

            pe.wait_ge(half_free[0], 3 * KF + 1)
            pe.wait_ge(half_free[1], 3 * KF + 1)
            for i in range(SLOTS):
                down(i, i % 2)
            with pe.Fori(1, ND // SLOTS) as g:
                for i in range(SLOTS):
                    down(g * SLOTS + i, i % 2)

        @block.scalar
        def _(act):
            act.dma_start(row[0:1, 0:D], b_qv.rearrange("(a n) -> a n", a=1)).then_inc(small_in, 16)
            for n, s in enumerate((g_xattn, g_ffn, b_sim)):
                act.dma_start(row[0:1, D + n:D + n + 1], s.rearrange("(a n) -> a n", a=1)).then_inc(small_in, 16)
            act.dma_start(wcol[:], wsim_v, allow_slow_non_contiguous=True).then_inc(small_in, 16)
            act.preload_act_table(ACT.Exp)
            act.wait_ge(rows_ps, 1)
            act.activation(c_t2, f_bank[0][:, D:D + 2], ACT.Tanh).then_inc(tanh_rdy, 1)

            def turned_h(b, s, proj):
                q = slice(s * PT, (s + 1) * PT)
                act.wait_ge(hT_ps, b * NP + s + 1)
                ge(act, pf_rdy, 4 * b)
                act.activation(hTf[:, :, q], tb_bank.rearrange("p (d n) -> p d n", d=KD), ACT.Copy).then_inc(hTf_rdy, 1)
                if proj:
                    act.wait_ge(f_ps, b * NP - NP + s + 1)
                act.wait_ge(hTf_rdy, b * NP + s + 1)
                act.activation(hth[:, :, q], hTf[:, :, q], ACT.Copy).then_inc(hth_rdy, 1)

            def turned_y(f, s):
                act.wait_ge(yT_ps, f * NP + s + 1)
                act.activation(yT[:, :, ds(f * S + s * PT, PT)], yb_bank.rearrange("p (d n) -> p d n", d=KD),
                               ACT.Copy).then_inc(yT_rdy, 1)

            def exps(b, s):
                act.wait_ge(nm_rdy, b * NP + s + 1)
                for t in range(2):
                    c = 2 * s + t
                    a_ = act.activation(sc[:, s % 2, t, :], sc[:, s % 2, t, :], ACT.Exp, bias=nm[:, c:c + 1],
                                        accum_out=rs[:, c:c + 1])
                a_.then_inc(exp_rdy, 1)

            def normed(b, s):
                act.wait_ge(ri_rdy, b * NP + s + 1)
                for t in range(2):
                    c = 2 * s + t
                    a_ = act.activation(sc[:, s % 2, t, :], sc[:, s % 2, t, :], ACT.Copy, scale=ri[:, c:c + 1])
                a_.then_inc(a_rdy, 1)

            def turned_a(b, s):
                act.wait_ge(at_ps, b * NP + s + 1)
                ge(act, hq_ps, 4 * b + (s // 2) * 2)
                act.activation(ath[0:JP, :, (s % 2) * PT:(s % 2 + 1) * PT],
                               ab_bank[0:JP, :].rearrange("p (k n) -> p k n", k=2), ACT.Copy).then_inc(ath_rdy, 1)

            def attended(b, hf, d):
                q = slice(hf * CH, (hf + 1) * CH)
                act.wait_ge(wml_rdy, 1)
                act.wait_ge(hq_ps, 4 * b + 2 * hf + d + 1)
                act.activation(hqh[:, d, q], hq_bank[d], ACT.Copy).then_inc(hqh_rdy, 1)

            def product(b, hf, d):
                q = slice(hf * CH, (hf + 1) * CH)
                act.wait_ge(pf_rdy, 4 * b + 2 * hf + d + 1)
                act.activation(prh[:, d, q], pf[:, d, :], ACT.Copy).then_inc(prh_rdy, 1)

            def turned_context(b):
                act.wait_ge(cxT_ps, b + 1)
                ge(act, cbi_ps, b)
                ge(act, cpf_rdy, b)
                act.activation(cxT[:], tb_bank[:, 0:2 * J].rearrange("p (d j) -> p d j", d=KD), ACT.Copy).then_inc(cxT_rdy, 1)

            def context_v(b):
                ge(act, hq_ps, 4 * b)
                act.wait_ge(cx_in, 16 * b + 16)
                act.activation(cxh[:], cx[:], ACT.Copy).then_inc(cxh_rdy, 1)

            def context_k(b):
                act.wait_ge(cpf_rdy, b + 1)
                ge(act, sc_ps, NP * b)
                act.activation(cph[:], cpf[:], ACT.Copy).then_inc(cph_rdy, 1)

            def scores(b, proj):
                f = b - 1
                for s in range(NP):
                    if not proj and s == NP - 1:
                        act.wait_ge(wqv_in, 48)
                        act.activation(wmh[:], wmid[:], ACT.Copy).then_inc(wmh_rdy, 1)
                    turned_h(b, s, proj)
                    if s >= 1:
                        exps(b, s - 1)
                        normed(b, s - 1)
                    if s >= 2:
                        turned_a(b, s - 2)
                    if proj and s >= 1:
                        turned_y(f, s - 1)
                exps(b, NP - 1)
                normed(b, NP - 1)
                attended(b, 0, 0)
                if proj:
                    turned_y(f, NP - 1)

            def summary(b, more):
                act.wait_ge(ngm_rdy, b + 1)
                act.activation(eb, rm, ACT.Exp, bias=c_ngm, accum_out=c_es).then_inc(eb_rdy, 1)
                attended(b, 0, 1)
                turned_a(b, 2)
                if more:
                    turned_context(b + 1)
                for d in range(KD):
                    product(b, 0, d)
                turned_a(b, 3)
                if more:
                    context_k(b + 1)
                attended(b, 1, 0)
                act.wait_ge(wef_rdy, b + 1)
                act.activation(weh[:], wef[:], ACT.Copy).then_inc(weh_rdy, 1)
                product(b, 1, 0)
                attended(b, 1, 1)
                product(b, 1, 1)
                if more:
                    context_v(b + 1)

            turned_context(0)
            context_v(0)
            context_k(0)
            scores(0, False)
            with act.Fori(1, B) as b:
                summary(b - 1, True)
                scores(b, True)
            summary(B - 1, False)
            f = B - 1

            def turned_w(m):
                for q in range(3):
                    act.wait_ge(wt_ps, 3 * m + q + 1)
                    act.activation(w_part(m, q, 0), w_seen(m, q), ACT.Copy).then_inc(wth_rdy, 1)

            for s in range(NP):
                if s < 3:
                    turned_w(s)
                if s >= 1:
                    turned_y(f, s - 1)
            turned_y(f, NP - 1)

            act.wait_ge(scales, 1)
            for c in range(NC):
                ge(act, xq_rdy, c - 1)
                act.activation(xqi[:, c % 2], yT[:, :, c * CH:(c + 1) * CH], ACT.Copy, scale=c_ix).then_inc(xqi_rdy, 1)
            act.wait_ge(x1_out, 16 * B)
            with act.Fori(0, KF) as k:
                for hf in range(2):
                    act.wait_ge(unit_ps, k * 2 + hf + 1)
                    act.activation(unit(hid, k, hf), ps_half(hf), ACT.Copy).then_inc(half_free[hf], 1)
            act.preload_act_table(ACT.Sigmoid)
            act.wait_ge(scales, 2)

            def gate_steps(k, hf):
                u = k * 2 + hf
                act.activation(unit(gq, k, hf), unit(hid, k, hf), ACT.Copy, scale=c_cg).then_inc(gq_rdy, 1)
                ge(act, p_rdy, u - 1)
                plain(act)
                act.activation(ag[:, hf, :], unit(hid, k, hf), ACT.Abs, scale=c_cg).then_inc(ag_rdy, 1)
                act.wait_ge(gq_rdy, u + 1)
                act.wait_ge(ag_rdy, u + 1)
                plain(act)
                act.activation(unit(hid, k, hf), unit(gq, k, hf), ACT.Sigmoid, scale=c_sg).then_inc(sig_rdy, 1)

            def up_steps(k, hf):
                u = k * 2 + hf
                ge(act, o_rdy, u - 1)
                act.activation(pq[hf][:], unit(hid, k, hf), ACT.Copy, scale=c_cp).then_inc(pq_rdy, 1)
                act.wait_ge(unit_ps, 2 * NU + u + 1)
                plain(act)
                act.activation(au[:, hf, :], ps_half(hf), ACT.Abs, scale=c_cu).then_inc(au_rdy, 1)

            def halves(steps):
                for hf in range(2):
                    steps(0, hf)
                with act.Fori(1, KF) as k:
                    for hf in range(2):
                        steps(k, hf)

            halves(gate_steps)
            act.wait_ge(scales, 3)
            for u in range(2):
                act.wait_ge(unit_ps, 2 * NU + u + 1)
                act.wait_ge(p_rdy, NU - 1 + u)
                act.activation(au[:, u, :], ps_half(u), ACT.Abs, scale=c_cu).then_inc(au_rdy, 1)
            act.wait_ge(scales, 4)
            for u in range(2):
                act.activation(pq[u][:], hid[:, 0, u * HALF:(u + 1) * HALF], ACT.Copy, scale=c_cp).then_inc(pq_rdy, 1)
            with act.Fori(1, KF) as k:
                for hf in range(2):
                    up_steps(k, hf)
            act.wait_ge(scales, 5)

            def product_q(c, par):
                ge(act, os_rdy, c - 1)
                act.activation(oq[:, par], hid[:, :, ds(c * CD, CD)], ACT.Copy, scale=c_co).then_inc(oqa_rdy, 1)

            for i in range(SLOTS):
                product_q(i, i % 2)
            with act.Fori(1, ND // SLOTS) as g:
                for i in range(SLOTS):
                    product_q(g * SLOTS + i, i % 2)

        @block.vector
        def _(dve):
            done = [0]

            def link(ins):
                done[0] += 1
                ins.then_inc(chain, 1)
                dve.wait_ge(chain, done[0])

            def stats(n, tiles):
                ge(dve, agg_done, n)
                ge(dve, mv_done, n)
                plain(dve)
                for t in range(TB):
                    i_ = dve.bn_stats(st[:, t, :], xa[:, ds(tiles + t, 1), :].rearrange("p a d -> p (a d)"))
                i_.then_inc(bn_done, 1)
                dve.wait_ge(bn_done, n + 1)
                plain(dve)
                for t in range(TB):
                    i_ = dve.bn_aggr(mvb[:, t, :], st[:, t, :])
                i_.then_inc(agg_done, 1)
                dve.wait_ge(agg_done, n + 1)
                dve.tensor_copy(mv[:, ds(tiles, TB), :], mvb).then_inc(mv_done, 1)

            def norm_x(b, s):
                for t in range(2):
                    g = b * TB + 2 * s + t
                    i_ = dve.tensor_scalar(h[:, 2 * s + t, :], xa[:, ds(g, 1), :].rearrange("p a d -> p (a d)"),
                                           mv[:, ds(g, 1), 0:1].rearrange("p a d -> p (a d)"), rstd[:, ds(g, 1)],
                                           ALU.subtract, ALU.mult)
                i_.then_inc(h_rdy, 1)

            def context_k(b):
                dve.wait_ge(cxT_rdy, b + 1)
                ge(dve, cp_rdy, b)
                for d in range(KD):
                    i_ = dve.tensor_scalar(cpf[:, d, :], cxT[:, d, :], wcol[:, 2 * KD + d:2 * KD + d + 1],
                                           wcol[:, d:d + 1], ALU.mult, ALU.add)
                i_.then_inc(cpf_rdy, 1)

            def context_bias(b):
                dve.wait_ge(cbi_ps, b + 1)
                dve.tensor_scalar(cbi[:], tb_bank[:, 2 * J:3 * J], c_bs, None, ALU.add).then_inc(cbi_rdy, 1)

            def scored(b, s):
                n = b * NP + s
                dve.wait_ge(sc_ps, n + 1)
                dve.wait_ge(cbi_rdy, b + 1)
                ge(dve, at_ps, n - 1)
                plain(dve)
                for t in range(2):
                    i_ = dve.tensor_tensor_reduce(sc[:, s % 2, t, :], sb_bank[:, t * J:(t + 1) * J], cbi[:], 1.0,
                                                  -3.4e38, ALU.add, ALU.max, rm[:, 2 * s + t:2 * s + t + 1])
                i_.then_inc(sc_rdy, 1)
                dve.wait_ge(sc_rdy, n + 1)
                dve.tensor_scalar(nm[:, 2 * s:2 * s + 2], rm[:, 2 * s:2 * s + 2], -1.0, None, ALU.mult).then_inc(nm_rdy, 1)

            def normed(b, s):
                dve.wait_ge(exp_rdy, b * NP + s + 1)
                dve.reciprocal(ri[:, 2 * s:2 * s + 2], rs[:, 2 * s:2 * s + 2]).then_inc(ri_rdy, 1)

            def turned_a(b, s):
                dve.wait_ge(ath_rdy, b * NP + s + 1)
                q = slice((s % 2) * PT, (s % 2 + 1) * PT)
                dve.tensor_tensor(atl[0:JP, :, q], ab_bank[0:JP, :].rearrange("p (k n) -> p k n", k=2),
                                  ath[0:JP, :, q].bitcast(F32), ALU.subtract).then_inc(at_rdy, 1)

            def attended(b, hf, d):
                q = slice(hf * CH, (hf + 1) * CH)
                n = b * 4 + hf * 2 + d
                dve.wait_ge(hqh_rdy, n + 1)
                dve.tensor_tensor(hql[:, d, q], hq_bank[d], hqh[:, d, q].bitcast(F32), ALU.subtract).then_inc(hql_rdy, 1)
                ge(dve, prl_rdy, n - 1 if hf else b * 4)
                dve.tensor_tensor(pf[:, d, :], hq_bank[d], hTf[:, d, q], ALU.mult).then_inc(pf_rdy, 1)

            def residual(f, s):
                n = f * NP + s
                g = f * TB + 2 * s
                dve.wait_ge(f_ps, n + 1)
                dve.wait_ge(xb_rdy, n + 1)
                x_ = xa[:, ds(g, 2), :]
                dve.scalar_tensor_tensor(x_, f_bank[s % 2].rearrange("p (t d) -> p t d", t=2), c_tx, x_,
                                         ALU.mult, ALU.add).then_inc(x1_rdy, 1)
                dve.wait_ge(x1_rdy, n + 1)
                plain(dve)
                for t in range(2):
                    i_ = dve.bn_stats(st[:, t, :], xa[:, ds(g + t, 1), :].rearrange("p a d -> p (a d)"))
                i_.then_inc(bn2_done, 1)
                dve.wait_ge(bn2_done, n + 1)
                plain(dve)
                for t in range(2):
                    i_ = dve.bn_aggr(mv2[:, t, :], st[:, t, :])
                i_.then_inc(mv2_done, 1)
                dve.wait_ge(mv2_done, n + 1)
                dve.tensor_scalar(vp2, mv2[:, :, 1], LN_EPS, None, ALU.add).then_inc(vp2_done, 1)

            def norm_x1(f, s):
                n = f * NP + s
                dve.wait_ge(rstd2_rdy, n + 1)
                ge(dve, yT_ps, f * NP + max(s - 1, 0))
                for t in range(2):
                    i_ = dve.tensor_scalar(yb[:, s % 2, t, :], xa[:, ds(f * TB + 2 * s + t, 1), :].rearrange("p a d -> p (a d)"),
                                           mv2[:, t, 0:1], rstd2[:, t:t + 1], ALU.subtract, ALU.mult)
                i_.then_inc(y_rdy, 1)
                dve.wait_ge(y_rdy, n + 1)
                dve.tensor_reduce(ymx[:, ds(n, 1)], yb[:, s % 2].rearrange("p t d -> p (t d)"), AX.X, ALU.max,
                                  apply_absolute_value=True).then_inc(ym_done, 1)

            WL = 8

            def wlink(m, i, ins):
                ins.then_inc(wchain, 1)
                dve.wait_ge(wchain, m * WL + i + 1)

            def weight_scales(m):
                ge(dve, wn_rdy, m)
                wlink(m, 0, dve.tensor_reduce(wsc[:], wr[:, ds(m, 1), :].rearrange("p a (n k) -> p (a n) k", k=QB),
                                              AX.X, ALU.max, apply_absolute_value=True))
                wlink(m, 1, dve.tensor_scalar(wsc[:], wsc[:], 1.0 / 7.0, EPS, ALU.mult, ALU.max))
                wlink(m, 2, dve.tensor_reduce(c_sm, wsc[:], AX.X, ALU.max))
                dve.reciprocal(wri[:], wsc[:]).then_inc(wmax_rdy, 1)

            def weight_unit(m):
                dve.wait_ge(wall_rdy, m + 1)
                wlink(m, 3, dve.tensor_scalar(c_pw.bitcast(I32), c_sa.bitcast(I32), 0x7F800000, None, ALU.bitwise_and))
                wlink(m, 4, dve.reciprocal(c_wt, c_pw))
                wlink(m, 5, dve.tensor_scalar(c_dn[:, ds(m, 1)], c_pw, 1.0 / W_SCALE, None, ALU.mult))
                wlink(m, 6, dve.tensor_scalar(wsc[:], wsc[:], c_wt, W_SCALE, ALU.mult, ALU.mult))

            def weight_values(m):
                dve.wait_ge(wq_rdy, m + 1)
                wm = wr[:, ds(m, 1), :].rearrange("p a n -> p (a n)")
                wlink(m, 7, dve.tensor_scalar(wqi[:], wm, 7.0, -8.0, ALU.min, ALU.max))
                dve.tensor_tensor(wm.rearrange("p (n k) -> p n k", k=QB), wqi[:].rearrange("p (n k) -> p n k", k=QB),
                                  wsc[:].unsqueeze(2).broadcast_to([P, NB, QB]), ALU.mult).then_inc(wn_rdy, 1)

            def weight_parts(m):
                for q in range(3):
                    dve.wait_ge(wth_rdy, 3 * m + q + 1)
                    dve.tensor_tensor(w_part(m, q, 1), w_seen(m, q), w_part(m, q, 0), ALU.subtract).then_inc(wt_rdy, 1)

            def row_stats(b):
                dve.wait_ge((x0_in, x1_in, x2_in, x3_in)[b], 16 * NP if b == 0 else 16)
                stats(b, b * TB)
                dve.wait_ge(mv_done, b + 1)
                t = slice(b * TB, (b + 1) * TB)
                dve.tensor_scalar(rstd[:, t], mv[:, t, 1], LN_EPS, None, ALU.add).then_inc(vp_done, 1)

            def scores(b, proj):
                f = b - 1
                for s in range(NP):
                    if proj:
                        if s == 0:
                            weight_values(b - 1)
                        residual(f, s)
                    elif s < B - 1:
                        row_stats(s + 1)
                    else:
                        dve.wait_ge(wmh_rdy, 1)
                        dve.tensor_tensor(wml[:], wmid[:], wmh[:].bitcast(F32), ALU.subtract).then_inc(wml_rdy, 1)
                    if s >= 1:
                        scored(b, s - 1)
                    if proj:
                        norm_x1(f, s)
                    if s >= 1:
                        normed(b, s - 1)
                    if s >= 2:
                        turned_a(b, s - 2)
                scored(b, NP - 1)
                dve.tensor_reduce(c_m1, rm, AX.X, ALU.max).then_inc(m1_rdy, 1)
                dve.wait_ge(m1_rdy, b + 1)
                dve.tensor_scalar(diag[:], ident[:], c_m1, None, ALU.mult).then_inc(diag_rdy, 1)
                normed(b, NP - 1)
                attended(b, 0, 0)

            def summary(b, more):
                dve.wait_ge(m_ps, b + 1)
                dve.tensor_reduce(c_ngm, sb_bank[:, 0:P], AX.X, ALU.max, negate=True).then_inc(ngm_rdy, 1)
                attended(b, 0, 1)
                turned_a(b, 2)
                if more:
                    context_k(b + 1)
                turned_a(b, 3)
                if more:
                    context_bias(b + 1)
                    weight_scales(b)
                dve.wait_ge(hrow_ps, b + 1)
                dve.reciprocal(c_rs, sb_bank[:, SUM:SUM + 1]).then_inc(crs_rdy, 1)
                dve.tensor_copy(hrow[0:1, :], sb_bank[0:1, P:P + D]).then_inc(hrow_rdy, 1)
                if more:
                    norm_x(b + 1, 0)
                dve.wait_ge(crs_rdy, b + 1)
                dve.wait_ge(hc_ps, b + 1)
                dve.tensor_scalar(c_hc, sb_bank[:, SUM + 1:SUM + 1 + KD], c_rs, None, ALU.mult).then_inc(hc_rdy, 1)
                dve.wait_ge(hc_rdy, b + 1)
                for d in range(KD):
                    i_ = dve.scalar_tensor_tensor(wef[:, d, :], w3[:, d, :], c_hc[:, d:d + 1], w0[:, d, :], ALU.mult, ALU.add)
                i_.then_inc(wef_rdy, 1)
                attended(b, 1, 0)
                dve.wait_ge(weh_rdy, b + 1)
                dve.tensor_tensor(wel[:], wef[:], weh[:].bitcast(F32), ALU.subtract).then_inc(we_rdy, 1)
                attended(b, 1, 1)
                if more:
                    for s in range(1, NP):
                        norm_x(b + 1, s)
                    weight_unit(b)

            row_stats(0)
            dve.wait_ge(ones_rdy, 1)
            dve.wait_ge(small_in, 80)
            for d in range(KD):
                dve.tensor_scalar(w2b[:, d, :], ones[:], wcol[:, KD + d:KD + d + 1], None, ALU.mult).then_inc(w2b_rdy, 1)
            dve.wait_ge(ident_rdy, 1)
            dve.wait_ge(rstd_rdy, 1)
            norm_x(0, 0)
            context_k(0)
            dve.wait_ge(tanh_rdy, 1)
            link(dve.tensor_copy(c_bs, f_bank[0][:, D + 2:D + 3]))
            context_bias(0)
            for s in range(1, NP):
                norm_x(0, s)
            dve.tensor_scalar(tgb[:], f_bank[0][:, 0:D], c_tx, None, ALU.mult).then_inc(tgb_rdy, 1)
            scores(0, False)
            dve.wait_ge(rstd_rdy, B)
            dve.wait_ge(wffn_in, 48)
            with dve.Fori(1, B) as b:
                summary(b - 1, True)
                scores(b, True)
            summary(B - 1, False)
            f = B - 1
            for s in range(NP):
                residual(f, s)
                norm_x1(f, s)
                if s < 3:
                    weight_parts(s)

            def largest(n, counts, m):
                dve.wait_ge(*counts)
                dve.tensor_reduce(c_loc[:, n:n + 1], m, AX.X, ALU.max).then_inc(loc_rdy, 1)

            def overall(n):
                dve.wait_ge(all_rdy, n + 1)
                return c_all[:, n:n + 1]

            largest(0, (ym_done, B * NP), ymx)
            v = overall(0)
            link(dve.tensor_scalar(c_sx, v, 1.0 / QMAX, EPS, ALU.mult, ALU.max))
            dve.reciprocal(c_ix, c_sx).then_inc(scales, 1)
            dve.wait_ge(yT_rdy, B * NP)
            dve.tensor_scalar(c_kg, c_sx, c_dn[:, 0:1], None, ALU.mult).then_inc(half_free[0], 1)
            dve.tensor_scalar(c_ku, c_sx, c_dn[:, 1:2], None, ALU.mult).then_inc(half_free[1], 1)
            dve.wait_ge(half_free[0], 1)
            dve.wait_ge(half_free[1], 1)
            dve.tensor_scalar(c_kgq, c_kg, 1.0 / QMAX, None, ALU.mult)
            dve.tensor_scalar(c_kuq, c_ku, 1.0 / QMAX, None, ALU.mult)
            link(dve.tensor_scalar(c_ft, c_tf, c_dn[:, 2:3], None, ALU.mult))
            for c in range(NC):
                dve.wait_ge(xqi_rdy, c + 1)
                n = slice(c * CH, (c + 1) * CH)
                dve.tensor_copy(xh[:, :, n], xqi[:, c % 2]).then_inc(xh_rdy, 1)
                dve.wait_ge(xh_rdy, c + 1)
                dve.tensor_tensor(xl[:, :, n], xqi[:, c % 2], xh[:, :, n], ALU.subtract).then_inc(xq_rdy, 1)
            with dve.Fori(0, KF) as k:
                for hf in range(2):
                    dve.wait_ge(half_free[hf], k + 2)
                    dve.tensor_reduce(gmx[:, ds(k * 2 + hf, 1)], unit(hid, k, hf), AX.X, ALU.max,
                                      apply_absolute_value=True).then_inc(gm_done, 1)
            largest(1, (gm_done, NU), gmx)
            v = overall(1)
            link(dve.tensor_scalar(c_sg, v, c_kgq, EPS, ALU.mult, ALU.max))
            link(dve.reciprocal(c_rg, c_sg))
            dve.tensor_scalar(c_cg, c_rg, c_kg, None, ALU.mult).then_inc(scales, 1)
            link(dve.tensor_scalar(c_kp, c_sg, 1.0 / 65536.0, None, ALU.mult))
            link(dve.tensor_scalar(c_kpq, c_kp, 1.0 / QMAX, None, ALU.mult))

            def up_max(u):
                dve.wait_ge(unit_ps, NU + u + 1)
                dve.tensor_reduce(umx[:, u:u + 1], ps_half(u % 2), AX.X, ALU.max,
                                  apply_absolute_value=True).then_inc(half_free[u % 2], 1)

            def gated(u):
                k, hf = u // 2, u % 2
                dve.wait_ge(sig_rdy, u + 1)
                ge(dve, p_rdy, u)
                dve.tensor_scalar(sq[:], hid[:, k, hf * HALF:(hf + 1) * HALF], 65536.0, None, ALU.mult).then_inc(sq_rdy, 1)
                dve.wait_ge(sq_rdy, u + 1)
                dve.wait_ge(ag_rdy, u + 1)
                dve.tensor_tensor_reduce(hid[:, k, hf * HALF:(hf + 1) * HALF], ag[:, hf, :], sq[:], 1.0, 0.0,
                                         ALU.mult, ALU.max, pmx[:, u:u + 1]).then_inc(p_rdy, 1)

            up_max(0)
            for u in range(1, NU):
                up_max(u)
                if u < NU - 1:
                    gated(u - 1)
            dve.wait_ge(half_free[1], 2 * KF + 1)
            largest(2, (half_free[0], 2 * KF + 1), umx)
            gated(NU - 2)
            v = overall(2)
            link(dve.tensor_scalar(c_su, v, c_kuq, EPS, ALU.mult, ALU.max))
            link(dve.reciprocal(c_ru, c_su))
            dve.tensor_scalar(c_cu, c_ru, c_ku, None, ALU.mult).then_inc(scales, 1)
            gated(NU - 1)
            largest(3, (p_rdy, NU), pmx)

            def product_sign(u):
                k, hf = u // 2, u % 2
                g_ = gq[:, k, hf * HALF:(hf + 1) * HALF]
                dve.wait_ge(au_rdy, u + 1)
                dve.tensor_tensor(g_.bitcast(BF16), g_, ps_half(hf), ALU.mult).then_inc(half_free[hf], 1)

            def product_max(u):
                k, hf = u // 2, u % 2
                dve.wait_ge(au_rdy, u + 1)
                dve.wait_ge(pq_rdy, u + 1)
                dve.tensor_tensor_reduce(hid[:, k, hf * HALF:(hf + 1) * HALF], pq[hf][:], au[:, hf, :], 1.0, 0.0,
                                         ALU.mult, ALU.max, omx[:, u:u + 1]).then_inc(o_rdy, 1)

            product_sign(0)
            v = overall(3)
            link(dve.tensor_scalar(c_sp, v, c_kpq, EPS, ALU.mult, ALU.max))
            link(dve.reciprocal(c_rp, c_sp))
            dve.tensor_scalar(c_cp, c_rp, c_kp, None, ALU.mult).then_inc(scales, 1)
            link(dve.tensor_scalar(c_ko, c_su, c_sp, None, ALU.mult))
            for u in range(NU):
                if 0 < u < NU - 1:
                    product_sign(u)
                product_max(u)
            largest(4, (o_rdy, NU), omx)
            product_sign(NU - 1)
            v = overall(4)
            link(dve.tensor_scalar(c_so, v, c_ko, 1.0 / QMAX, ALU.mult, ALU.mult))
            link(dve.tensor_scalar(c_so, c_so, EPS, None, ALU.max))
            link(dve.reciprocal(c_ro, c_so))
            dve.tensor_scalar(c_co, c_ro, c_ko, None, ALU.mult).then_inc(scales, 1)
            link(dve.tensor_scalar(c_fin, c_so, c_ft, None, ALU.mult))
            for hf in range(2):
                dve.wait_ge(half_free[hf], 3 * KF + 1)

            def signed(c, par):
                sg = gq[:, :, ds(c * CD, CD)].bitcast(BF16)
                dve.tensor_scalar(sg, sg, 1.0, -1.0, ALU.min, ALU.max).then_inc(sgn_rdy, 1)
                dve.wait_ge(oqa_rdy, c + 1)
                dve.wait_ge(sgn_rdy, c + 1)
                dve.tensor_tensor(oq[:, par], oq[:, par], sg, ALU.mult).then_inc(oqs_rdy, 1)
                dve.wait_ge(oqs_rdy, c + 1)
                ge(dve, dn_ps, c - 1)
                dve.tensor_copy(oh[:, par], oq[:, par]).then_inc(oh_rdy, 1)
                dve.wait_ge(oh_rdy, c + 1)
                dve.tensor_tensor(ol[:, par], oq[:, par], oh[:, par], ALU.subtract).then_inc(os_rdy, 1)

            def final(g, i):
                dve.wait_ge(dn_ps, g * SLOTS + i + 1)
                dve.wait_ge(xo_in[i], g * 16 + 16)
                y_ = xo[:, i].rearrange("p t d -> p (t d)")
                dve.scalar_tensor_tensor(y_, ps[i % 2][:, 0, :], c_fin, y_, ALU.mult, ALU.add).then_inc(fin_rdy, 1)

            for i in range(SLOTS):
                signed(i, i % 2)
                if i >= 1:
                    final(0, i - 1)
            with dve.Fori(1, ND // SLOTS) as g:
                for i in range(SLOTS):
                    signed(g * SLOTS + i, i % 2)
                    if i == 0:
                        final(g - 1, SLOTS - 1)
                    else:
                        final(g, i - 1)
            final(ND // SLOTS - 1, SLOTS - 1)


_INS = ["x", "ctx_1024", "g_xattn", "g_ffn", "L0_xattn_w_sim", "L0_xattn_b_sim", "L0_xattn_W_qv", "L0_xattn_b_qv",
        "L0_ffn_w_gate", "L0_ffn_w_up", "L0_ffn_w_down"]


def kernel(**inputs):
    import numpy as _np
    import concourse.bacc as _bacc
    from concourse.bass_utils import run_bass_kernel_spmd as _run

    nc = _bacc.Bacc("TRN2", target_bir_lowering=False, num_devices=1)
    arrays, args = {}, []
    for name in _INS:
        v = _np.ascontiguousarray(inputs[name])
        arrays[f"in_{name}"] = v
        args.append(nc.dram_tensor(f"in_{name}", v.shape, mybir.dt.from_np(v.dtype), kind="ExternalInput").ap())
    out = nc.dram_tensor("out_dram", (B, S, D), F32, kind="ExternalOutput").ap()
    build(nc, *args, out)
    r = _run(nc, [arrays], core_ids=[0])
    return r.results[0]["out_dram"]
```

```python
from contextlib import ExitStack

import concourse.bass as bass
from concourse import mybir
from concourse.alu_op_type import AluOpType as ALU

F32 = mybir.dt.float32
F32R = mybir.dt.float32r
F16 = mybir.dt.float16
BF16 = mybir.dt.bfloat16
I16 = mybir.dt.int16
U16 = mybir.dt.uint16
I32 = mybir.dt.int32
ACT = mybir.ActivationFunctionType
AX = mybir.AxisListType
RMAX = bass.bass_isa.ReduceOp.max
ds = bass.ds

P = 128
B, S, D = 4, 1024, 256
J = 154
JP = J // 2
FF = 768
KD = D // P
KF = FF // P
TOK = B * S
TB = S // P
NP = TB // 2
PT = 2 * P
HALF = TOK // 2
NU = 2 * KF
CH = 512
NC = TOK // CH
CD = 256
ND = TOK // CD
SLOTS = 4
QB = 32
NB = FF * D // P // QB
WE = FF * D // P
QMAX = 32767.0
EPS = 1e-12
LN_EPS = 1e-5
COLS = 320
W_SCALE = 2.0 ** 11


def build(nc, x, ctx, g_xattn, g_ffn, w_sim, b_sim, w_qv, b_qv, w_gate, w_up, w_down, out):
    x1_dram = nc.dram_tensor("x1_scratch", (TOK, D), F32, kind="Internal").ap()

    base = -(-nc.sbuf_base // 64) * 64
    top = [base]

    def region(size):
        at = top[0]
        top[0] += -(-size // 32) * 32
        assert top[0] <= nc.sbuf_usable_end, (top[0], nc.sbuf_usable_end)
        return [at, at + size]

    def place(where, name, shape, dt, size_of={F32: 4, F32R: 4, I32: 4, F16: 2, BF16: 2, I16: 2, U16: 2}):
        n = size_of[dt]
        for k in shape[1:]:
            n *= k
        at = where[0]
        where[0] += -(-n // 32) * 32
        assert where[0] <= where[1], (name, where)
        return nc.alloc_sbuf_tensor_at(name, shape, dt, offset=at)

    r_hid = region(KF * TOK * 4)
    r_sgn = region(KF * TOK * 2)
    r_x = region(2 * KD * TOK * 2)
    r_wg = region(2 * KD * FF * 2)
    r_wu = region(2 * KD * FF * 2)
    r_wd = region(2 * KF * D * 2)
    r_tmp = region(12288)
    r_own = region(512 + 1280)

    def copy_of(r):
        return [r[0], r[1]]

    ident = place(r_own, "ident", [P, P], F32)
    cols = place(r_own, "cols", [P, COLS], F32)
    used = [0]

    def col(n=1):
        used[0] += n
        assert used[0] <= COLS
        return cols[:, used[0] - n:used[0]]

    hid = place(copy_of(r_hid), "hid", [P, KF, TOK], F32)
    gq = place(copy_of(r_sgn), "gq", [P, KF, TOK], I16)
    a = copy_of(r_x)
    xh = place(a, "xh", [P, KD, TOK], F16)
    xl = place(a, "xl", [P, KD, TOK], F16)
    a = copy_of(r_wg)
    wgh = place(a, "wgh", [P, KD, FF], F16)
    wgl = place(a, "wgl", [P, KD, FF], F16)
    a = copy_of(r_wu)
    wuh = place(a, "wuh", [P, KD, FF], F16)
    wul = place(a, "wul", [P, KD, FF], F16)
    a = copy_of(r_wd)
    wdh = place(a, "wdh", [P, KF, D], F16)
    wdl = place(a, "wdl", [P, KF, D], F16)
    a = copy_of(r_tmp)
    ag = place(a, "ag", [P, 2, HALF], I16)
    sq = place(a, "sq", [P, HALF], U16)
    a = copy_of(r_tmp)
    au = place(a, "au", [P, 2, HALF], I16)
    pq = [place(a, "pq0", [P, HALF], I16), place(copy_of(r_wg), "pq1", [P, HALF], I16)]
    oq = place(copy_of(r_tmp), "oq", [P, 2, KF, CD], I16)
    a = copy_of(r_x)
    oh = place(a, "oh", [P, 2, KF, CD], F16)
    ol = place(a, "ol", [P, 2, KF, CD], F16)
    xo = place([r_wg[0], r_wu[1]], "xo", [P, SLOTS, CD // P, D], F32)

    a = copy_of(r_sgn)
    yT = place(a, "yT", [P, KD, TOK], F32)
    xqi = place(copy_of(a), "xqi", [P, 2, KD, CH], I16)
    hTf = place(a, "hTf", [P, KD, S], F32)
    y_last = r_sgn[0] + (TOK - S) * 4
    ath = [place(a, "ath0", [JP, 2, CH], F32R), place([y_last, y_last + S * 4], "ath1", [JP, 2, CH], F32R)]
    y_last += TOK * 4
    atl = [place(a, "atl0", [JP, 2, CH], F32R), place([y_last, y_last + S * 4], "atl1", [JP, 2, CH], F32R)]
    a = copy_of(r_hid)
    xa = place(a, "xa", [P, B * TB, D], F32)
    hth = place(a, "hth", [P, KD, S], F32R)
    htl = place(a, "htl", [P, KD, S], F32R)
    wmid = place(copy_of(a), "wmid", [P, 2 * KD, D], F32)
    hqh = place(a, "hqh", [P, KD, S], F32R)
    hql = place(a, "hql", [P, KD, S], F32R)
    prh = place(a, "prh", [P, KD, S], F32R)
    prl = place(a, "prl", [P, KD, S], F32R)
    wmh = place(a, "wmh", [P, 2 * KD, D], F32R)
    wml = place(a, "wml", [P, 2 * KD, D], F32R)
    weh = place(a, "weh", [P, KD, D], F32R)
    wel = place(a, "wel", [P, KD, D], F32R)
    w0 = place(a, "w0", [P, KD, D], F32)
    w3 = place(a, "w3", [P, KD, D], F32)
    a = copy_of(r_x)
    wr = place(a, "wr", [P, 3, WE], F32)
    h = place(a, "h", [P, TB, D], F32)
    wqi = place(a, "wqi", [P, WE], I16)
    wsc = place(a, "wsc", [P, NB], F32)
    wri = place(a, "wri", [P, NB], F32)
    a = [r_wg[0], r_wd[1]]
    cx = place(a, "cx", [JP, 2, D], F32)
    cxh = place(a, "cxh", [JP, 2, D], F32R)
    cxl = place(a, "cxl", [JP, 2, D], F32R)
    cxT = place(a, "cxT", [P, KD, J], F32)
    cpf = place(a, "cpf", [P, KD, J], F32)
    cph = place(a, "cph", [P, KD, J], F32R)
    cpl = place(a, "cpl", [P, KD, J], F32R)
    cbi = place(a, "cbi", [P, J], F32)
    wef = place(a, "wef", [P, KD, D], F32)
    w2b = place(a, "w2b", [P, KD, P], F32)
    ones = place(a, "ones", [P, P], F32)
    diag = place(a, "diag", [P, P], F32)
    row = place(a, "row", [1, D + 3], F32)
    hrow = place(a, "hrow", [1, D], F32)
    wcol = place(a, "wcol", [P, 3 * KD], F32)
    a = copy_of(r_tmp)
    yb = place(a, "yb", [P, 2, 2, D], F32)
    sc = place(a, "sc", [P, 2, 2, J], F32)
    pf = place(a, "pf", [P, 2, CH], F32)
    tgb = place(a, "tgb", [P, D], F32)
    st = place(a, "st", [P, TB, 6], F32)

    mv = col(2 * TB).rearrange("p (t s) -> p t s", s=2)
    rstd, nmr = col(TB), col(TB)
    mhalf = col(TB)
    mv2 = col(4).rearrange("p (t s) -> p t s", s=2)
    vp2, rstd2 = col(2), col(2)
    rm, nm = col(TB), col(TB)
    rs, ri = col(TB), col(TB)
    eb = col(TB)
    ymx = col(B * NP)
    gmx, umx, pmx, omx = col(NU), col(NU), col(NU), col(NU)
    c_m1, c_ngm, c_es, c_rs, c_hc = col(), col(), col(), col(), col(KD)
    c_t2 = col(2)
    c_tx, c_tf = c_t2[:, 0:1], c_t2[:, 1:2]
    c_bs = col()
    c_sm, c_sa, c_pw, c_wt, c_dn = col(), col(), col(), col(), col(3)
    c_loc, c_all = col(5), col(5)
    c_sx, c_ix, c_kg, c_kgq, c_ku, c_kuq = (col() for _ in range(6))
    c_sg, c_rg, c_cg, c_kp, c_kpq = (col() for _ in range(5))
    c_su, c_ru, c_cu, c_sp, c_rp, c_cp = (col() for _ in range(6))
    c_ko, c_so, c_ro, c_co, c_ft, c_fin = (col() for _ in range(6))

    SUM = P + D + 8
    ps = [nc.alloc_psum_tensor(f"ps{i}", [P, 4, 512], F32) for i in range(2)]
    tb_bank, sb_bank, ab_bank, yb_bank = ps[0][:, 0, :], ps[0][:, 1, :], ps[0][:, 2, :], ps[0][:, 3, :]
    hq_bank = [ps[1][:, 0, :], ps[1][:, 1, :]]
    s_bank = [sb_bank, hq_bank[1]]
    f_bank = [ps[1][:, 2, :], ps[1][:, 3, :]]

    x_v = x.rearrange("b (t p) d -> p (b t) d", p=P)
    ctx_v = ctx.rearrange("b (k p) d -> b p k d", p=JP)
    wqv_v = w_qv.rearrange("(k p) n -> p k n", p=P)
    wsim_v = w_sim.rearrange("(k p) -> p k", p=P)
    x1_v = x1_dram.rearrange("(t p) d -> p t d", p=P)
    out_v = out.rearrange("b (t p) d -> p (b t) d", p=P)

    with ExitStack() as stack:
        def sem(name):
            return stack.enter_context(nc.semaphore(name))

        x0_in, xr_in, cx_in, small_in, wqv_in, wffn_in = map(sem, ("x0_in", "xr_in", "cx_in", "small_in", "wqv_in", "wffn_in"))
        x1_out = sem("x1_out")
        xo_in = [sem(f"xo_in{i}") for i in range(SLOTS)]
        out_out = [sem(f"out_out{i}") for i in range(SLOTS)]
        const_a, ident_rdy, mhalf_rdy, ones_rdy, rows_ps, tanh_rdy, tgb_rdy, w2b_rdy, wmh_rdy, wml_rdy = map(
            sem, ("const_a", "ident_rdy", "mhalf_rdy", "ones_rdy", "rows_ps", "tanh_rdy", "tgb_rdy", "w2b_rdy", "wmh_rdy", "wml_rdy"))
        bn_done, mv_done, vp_done, rstd_rdy, nmr_rdy, h_rdy, xb_rdy = map(sem, ("bn_done", "mv_done", "vp_done", "rstd_rdy", "nmr_rdy", "h_rdy", "xb_rdy"))
        cxT_ps, cxT_rdy, cbi_ps, cbi_rdy, cpf_rdy, cph_rdy, cp_rdy, cxh_rdy, cx_rdy = map(
            sem, ("cxT_ps", "cxT_rdy", "cbi_ps", "cbi_rdy", "cpf_rdy", "cph_rdy", "cp_rdy", "cxh_rdy", "cx_rdy"))
        hT_ps, hTf_rdy, hth_rdy, htl_rdy = map(sem, ("hT_ps", "hTf_rdy", "hth_rdy", "htl_rdy"))
        sc_ps, sc_rdy, nm_rdy, exp_rdy, ri_rdy, a_rdy = map(sem, ("sc_ps", "sc_rdy", "nm_rdy", "exp_rdy", "ri_rdy", "a_rdy"))
        at_ps, ath_rdy, at_rdy = map(sem, ("at_ps", "ath_rdy", "at_rdy"))
        hq_ps, hqh_rdy, hql_rdy, pf_rdy, prh_rdy, prl_rdy = map(sem, ("hq_ps", "hqh_rdy", "hql_rdy", "pf_rdy", "prh_rdy", "prl_rdy"))
        m1_rdy, diag_rdy, m_ps, ngm_rdy, eb_rdy, hrow_ps, hrow_rdy, hc_ps, crs_rdy, hc_rdy = map(
            sem, ("m1_rdy", "diag_rdy", "m_ps", "ngm_rdy", "eb_rdy", "hrow_ps", "hrow_rdy", "hc_ps", "crs_rdy", "hc_rdy"))
        wef_rdy, weh_rdy, we_rdy = map(sem, ("wef_rdy", "weh_rdy", "we_rdy"))
        f_ps, x1_rdy, bn2_done, mv2_done, vp2_done, rstd2_rdy, y_rdy, ym_done, yT_ps, yT_rdy = map(
            sem, ("f_ps", "x1_rdy", "bn2_done", "mv2_done", "vp2_done", "rstd2_rdy", "y_rdy", "ym_done", "yT_ps", "yT_rdy"))
        wchain, wmax_rdy, wall_rdy, wq_rdy, wqi_rdy, wqf_rdy, wn_rdy, wt_ps, wth_rdy, wt_rdy = map(
            sem, ("wchain", "wmax_rdy", "wall_rdy", "wq_rdy", "wqi_rdy", "wqf_rdy", "wn_rdy", "wt_ps", "wth_rdy", "wt_rdy"))
        loc_rdy, all_rdy, chain, scales = map(sem, ("loc_rdy", "all_rdy", "chain", "scales"))
        xqi_rdy, xh_rdy, xq_rdy, unit_ps, gm_done = map(sem, ("xqi_rdy", "xh_rdy", "xq_rdy", "unit_ps", "gm_done"))
        half_free = [sem("half0_free"), sem("half1_free")]
        gq_rdy, ag_rdy, sig_rdy, sq_rdy, p_rdy, pq_rdy, au_rdy, o_rdy = map(
            sem, ("gq_rdy", "ag_rdy", "sig_rdy", "sq_rdy", "p_rdy", "pq_rdy", "au_rdy", "o_rdy"))
        oqa_rdy, sgn_rdy, oqs_rdy, oh_rdy, os_rdy, dn_ps, fin_rdy = map(
            sem, ("oqa_rdy", "sgn_rdy", "oqs_rdy", "oh_rdy", "os_rdy", "dn_ps", "fin_rdy"))

        passed = sem("passed")

        block = stack.enter_context(nc.Block())

        def unit(t, k, hf):
            return t[:, ds(k, 1), hf * HALF:(hf + 1) * HALF].rearrange("p a n -> p (a n)")

        def ps_half(hf):
            return ps[hf][:].rearrange("p a n -> p (a n)")

        w_banks = [[tb_bank, sb_bank, ab_bank]] * 2 + [[*hq_bank, f_bank[0]]]

        def w_part(m, q, low):
            if m == 2:
                return (wdh, wdl)[low][:, 2 * q:2 * q + 2, :].rearrange("p k n -> p (k n)")
            return ((wgh, wgl), (wuh, wul))[m][low][:, :, q * D:(q + 1) * D]

        def w_seen(m, q):
            return w_banks[m][q] if m == 2 else w_banks[m][q].rearrange("p (k n) -> p k n", k=KD)

        def ge(eng, s, n):
            if not isinstance(n, int) or n > 0:
                eng.wait_ge(s, n)

        def plain(eng):
            eng.sem_inc(passed, 1)

        @block.sync
        def _(sp):
            for t in range(0, TB, 2):
                sp.dma_start(xa[:, t:t + 2, :], x_v[:, t:t + 2, :]).then_inc(x0_in, 16)
            sp.dma_start(cx[:], ctx_v[0]).then_inc(cx_in, 16)
            sp.dma_start(wmid[:], wqv_v[:, KD:3 * KD, :]).then_inc(wqv_in, 16)
            sp.dma_start(w0[:], wqv_v[:, 0:KD, :]).then_inc(wqv_in, 16)
            sp.dma_start(w3[:], wqv_v[:, 3 * KD:4 * KD, :]).then_inc(wqv_in, 16)
            for b in range(1, B):
                sp.dma_start(xa[:, b * TB:(b + 1) * TB, :], x_v[:, b * TB:(b + 1) * TB, :]).then_inc(xr_in, 16)
            for m, w in enumerate((w_gate, w_up)):
                sp.dma_start(wr[:, m, :].rearrange("p (k n) -> p k n", n=D),
                             w.rearrange("(k p) n -> p k n", p=P)).then_inc(wffn_in, 16)
            sp.dma_start(wr[:, 2, :].rearrange("p (k n) -> p k n", n=FF),
                         w_down.rearrange("(k p) n -> p k n", p=P)).then_inc(wffn_in, 16)
            with sp.Fori(1, B) as b:
                sp.wait_ge(cxT_ps, b)
                sp.wait_ge(cx_rdy, b)
                sp.dma_start(cx[:], ctx_v[ds(b, 1)].rearrange("b p k d -> p (b k) d")).then_inc(cx_in, 16)
            with sp.Fori(0, B) as b:
                sp.wait_ge(x1_rdy, b * NP + NP)
                sp.dma_start(x1_v[:, ds(b * TB, TB), :], xa[:, ds(b * TB, TB), :]).then_inc(x1_out, 16)
            sp.wait_ge(x1_out, 16 * B)
            sp.wait_ge(unit_ps, 3 * NU)
            sp.wait_ge(o_rdy, NU)
            for i in range(SLOTS):
                sp.dma_start(xo[:, i], x1_v[:, 2 * i:2 * i + 2, :]).then_inc(xo_in[i], 16)

            def store(g, i):
                sp.wait_ge(fin_rdy, g * SLOTS + i + 1)
                sp.dma_start(out_v[:, ds((g * SLOTS + i) * 2, 2), :], xo[:, i]).then_inc(out_out[i], 16)

            with sp.Fori(0, ND // SLOTS - 1) as g:
                for i in range(SLOTS):
                    store(g, i)
                    sp.wait_ge(out_out[i], g * 16 + 16)
                    sp.dma_start(xo[:, i], x1_v[:, ds(((g + 1) * SLOTS + i) * 2, 2), :]).then_inc(xo_in[i], 16)
            for i in range(SLOTS):
                store(ND // SLOTS - 1, i)
            for i in range(SLOTS):
                sp.wait_ge(out_out[i], 16 * (ND // SLOTS))

        @block.gpsimd
        def _(pool):
            pool.memset(ident[:], 0.0).then_inc(const_a, 1)
            pool.memset(mhalf, -0.5).then_inc(mhalf_rdy, 1)
            pool.memset(ones[:], 1.0).then_inc(ones_rdy, 1)
            pool.wait_ge(const_a, 1)
            pool.affine_select(out=ident[:], in_=ident[:], compare_op=ALU.not_equal, fill=1.0, base=0,
                               pattern=[[-1, P]], channel_multiplier=1).then_inc(ident_rdy, 1)

            def row_std(b):
                pool.wait_ge(vp_done, b + 1)
                pool.tensor_tensor(rstd, rstd, mhalf, ALU.pow).then_inc(rstd_rdy, 1)

            def context_v(b):
                pool.wait_ge(cxh_rdy, b + 1)
                pool.tensor_tensor(cxl[:], cx[:], cxh[:].bitcast(F32), ALU.subtract).then_inc(cx_rdy, 1)

            def context_k(b):
                pool.wait_ge(cph_rdy, b + 1)
                pool.tensor_tensor(cpl[:], cpf[:], cph[:].bitcast(F32), ALU.subtract).then_inc(cp_rdy, 1)

            def product(b, hf):
                for d in range(KD):
                    pool.wait_ge(prh_rdy, b * 4 + hf * 2 + d + 1)
                    q = slice(hf * CH, (hf + 1) * CH)
                    pool.tensor_tensor(prl[:, d, q], pf[:, d, :], prh[:, d, q].bitcast(F32), ALU.subtract).then_inc(prl_rdy, 1)

            def y_std(f, s):
                pool.wait_ge(vp2_done, f * NP + s + 1)
                pool.tensor_tensor(rstd2, vp2, mhalf[:, 0:2], ALU.pow).then_inc(rstd2_rdy, 1)

            def weight_q(m, i):
                if i == 0:
                    pool.wait_ge(wmax_rdy, m + 1)
                    plain(pool)
                    pool.partition_all_reduce(c_sa, c_sm, P, RMAX).then_inc(wall_rdy, 1)
                n = slice(i * NB // 2, (i + 1) * NB // 2)
                wm = wr[:, ds(m, 1), :].rearrange("p a (n k) -> p (a n) k", k=QB)[:, n, :]
                pool.tensor_tensor(wm, wm, wri[:, n].unsqueeze(2).broadcast_to([P, NB // 2, QB]), ALU.mult).then_inc(wq_rdy, 1)

            def weight_n(m):
                pool.wait_ge(wqf_rdy, m + 1)
                plain(pool)
                wm = wr[:, ds(m, 1), :].rearrange("p a (n k) -> p (a n) k", k=QB)
                pool.tensor_tensor(wm, wm, wsc[:].unsqueeze(2).broadcast_to([P, NB, QB]), ALU.mult).then_inc(wn_rdy, 1)

            def scores(b, proj):
                for s in range(NP):
                    pool.wait_ge(hth_rdy, b * NP + s + 1)
                    q = slice(s * PT, (s + 1) * PT)
                    pool.tensor_tensor(htl[:, :, q], hTf[:, :, q], hth[:, :, q].bitcast(F32), ALU.subtract).then_inc(htl_rdy, 1)
                    if proj:
                        y_std(b - 1, s)
                    pool.wait_ge(h_rdy, b * NP + s + 1)
                    t = ds(b * TB + 2 * s, 2)
                    pool.tensor_tensor(xa[:, t, :], xa[:, t, :], tgb[:].unsqueeze(1).broadcast_to([P, 2, D]), ALU.add).then_inc(xb_rdy, 1)
                    if proj and s < 2:
                        weight_q(b - 1, s)
                if proj:
                    weight_n(b - 1)

            pool.wait_ge(mhalf_rdy, 1)
            row_std(0)
            context_v(0)
            context_k(0)
            pool.wait_ge(tgb_rdy, 1)
            scores(0, False)
            with pool.Fori(1, B) as b:
                product(b - 1, 0)
                context_k(b)
                row_std(b)
                product(b - 1, 1)
                context_v(b)
                scores(b, True)
            product(B - 1, 0)
            product(B - 1, 1)
            for s in range(NP):
                y_std(B - 1, s)
            for n in range(5):
                pool.wait_ge(loc_rdy, n + 1)
                pool.partition_all_reduce(c_all[:, n:n + 1], c_loc[:, n:n + 1], P, RMAX).then_inc(all_rdy, 1)

        @block.tensor
        def _(pe):
            def three(dst, pairs, first=True, last=True):
                n = 3 * len(pairs)
                i = 0
                for sh, sl, mh, ml in pairs:
                    for st_, mo in ((sh, mh), (sl, mh), (sh, ml)):
                        mm = pe.matmul(dst, st_, mo, start=first and i == 0, stop=last and i == n - 1)
                        i += 1
                return mm

            def turn_context(b):
                pe.wait_ge(cx_in, 16 * b + 16)
                ge(pe, hTf_rdy, b * NP)
                for k in range(2):
                    for d in range(KD):
                        tr = pe.transpose(tb_bank[:, d * J + k * JP:d * J + (k + 1) * JP],
                                          cx[0:JP, k, d * P:(d + 1) * P], ident[0:JP, 0:JP])
                tr.then_inc(cxT_ps, 1)

            def context_bias(b):
                pe.wait_ge(cxT_rdy, b + 1)
                for d in range(KD):
                    mm = pe.matmul(tb_bank[:, 2 * J:3 * J], w2b[:, d, :], cxT[:, d, :], start=(d == 0), stop=(d == KD - 1))
                mm.then_inc(cbi_ps, 1)

            def turn_h(b, s):
                pe.wait_ge(h_rdy, b * NP + s + 1)
                if s == 0:
                    pe.wait_ge(cbi_rdy, b + 1)
                else:
                    pe.wait_ge(hTf_rdy, b * NP + s)
                for d in range(KD):
                    for t in range(2):
                        tr = pe.transpose(tb_bank[:, d * PT + t * P:d * PT + (t + 1) * P],
                                          h[:, 2 * s + t, d * P:(d + 1) * P], ident[:])
                tr.then_inc(hT_ps, 1)

            def project(f, s):
                pe.wait_ge(hql_rdy, f * 4 + (s // 2) * 2 + 2)
                pe.wait_ge(prl_rdy, f * 4 + (s // 2) * 2 + 2)
                if s >= 2:
                    pe.wait_ge(x1_rdy, f * NP + s - 1)
                for t in range(2):
                    q = slice(s * PT + t * P, s * PT + (t + 1) * P)
                    parts = [(hqh[:, d, q], hql[:, d, q], wmh[:, d, :], wml[:, d, :]) for d in range(KD)]
                    parts += [(prh[:, d, q], prl[:, d, q], wmh[:, KD + d, :], wml[:, KD + d, :]) for d in range(KD)]
                    three(f_bank[s % 2][:, t * D:(t + 1) * D], parts, last=False)
                    pe.wait_ge(we_rdy, f + 1)
                    parts = [(hth[:, d, q], htl[:, d, q], weh[:, d, :], wel[:, d, :]) for d in range(KD)]
                    mm = three(f_bank[s % 2][:, t * D:(t + 1) * D], parts, first=False)
                mm.then_inc(f_ps, 1)

            def turn_y(f, s):
                pe.wait_ge(y_rdy, f * NP + s + 1)
                if s >= 1:
                    pe.wait_ge(yT_rdy, f * NP + s)
                for d in range(KD):
                    for t in range(2):
                        tr = pe.transpose(yb_bank[:, d * PT + t * P:d * PT + (t + 1) * P],
                                          yb[:, s % 2, t, d * P:(d + 1) * P], ident[:])
                tr.then_inc(yT_ps, 1)

            def score(b, s):
                pe.wait_ge(htl_rdy, b * NP + s + 1)
                if s == 0:
                    pe.wait_ge(cp_rdy, b + 1)
                    ge(pe, hc_rdy, b)
                elif s == 1:
                    ge(pe, pf_rdy, b * 4)
                else:
                    pe.wait_ge(sc_rdy, b * NP + s - 1)
                for t in range(2):
                    q = slice(s * PT + t * P, s * PT + (t + 1) * P)
                    mm = three(s_bank[s % 2][:, t * J:(t + 1) * J],
                               [(hth[:, d, q], htl[:, d, q], cph[:, d, :], cpl[:, d, :]) for d in range(KD)])
                mm.then_inc(sc_ps, 1)

            def turn_a(b, s):
                pe.wait_ge(a_rdy, b * NP + s + 1)
                ge(pe, at_rdy, b * NP + s)
                for k in range(2):
                    for t in range(2):
                        tr = pe.transpose(ab_bank[0:JP, k * PT + t * P:k * PT + (t + 1) * P],
                                          sc[:, s % 2, t, k * JP:(k + 1) * JP], ident[:])
                tr.then_inc(at_ps, 1)

            def attend(b, hf, d):
                if hf == 0 and d == 1:
                    pe.wait_ge(sc_rdy, b * NP + NP)
                if d == 0:
                    pe.wait_ge(at_rdy, b * NP + 2 * hf + 2)
                    pe.wait_ge(cx_rdy, b + 1)
                if hf == 1:
                    pe.wait_ge(pf_rdy, b * 4 + 1 + d)
                mm = three(hq_bank[d], [(cxh[0:JP, k, d * P:(d + 1) * P], cxl[0:JP, k, d * P:(d + 1) * P],
                                         ath[hf][0:JP, k, :], atl[hf][0:JP, k, :]) for k in range(2)])
                mm.then_inc(hq_ps, 1)

            def batch_max(b):
                pe.wait_ge(diag_rdy, b + 1)
                pe.wait_ge(sc_rdy, b * NP + NP)
                pe.matmul(sb_bank[:, 0:P], ones[:], diag[:], start=True, stop=True).then_inc(m_ps, 1)

            def batch_sum(b):
                pe.wait_ge(eb_rdy, b + 1)
                for t in range(TB):
                    pe.matmul(sb_bank[0:1, P:P + D], eb[:, t:t + 1], h[:, t, :], start=(t == 0), stop=(t == TB - 1))
                pe.matmul(sb_bank[:, SUM:SUM + 1], ones[:], c_es, start=True, stop=True).then_inc(hrow_ps, 1)

            def batch_cols(b):
                pe.wait_ge(hrow_rdy, b + 1)
                pe.wait_ge(crs_rdy, b + 1)
                for d in range(KD):
                    mm = pe.matmul(sb_bank[:, SUM + 1 + d:SUM + 2 + d], hrow[0:1, d * P:(d + 1) * P], ones[0:1, 0:1],
                                   start=True, stop=True)
                mm.then_inc(hc_ps, 1)

            def scores(b, proj):
                f = b - 1
                for s in range(NP):
                    if proj:
                        project(f, s)
                    turn_h(b, s)
                    if proj and s >= 2:
                        turn_a(b, s - 2)
                    if s >= 1:
                        score(b, s - 1)
                    if not proj and s >= 2:
                        turn_a(b, s - 2)
                    if proj and s >= 1:
                        turn_y(f, s - 1)
                score(b, NP - 1)
                attend(b, 0, 0)
                turn_a(b, NP - 2)
                batch_max(b)
                if proj:
                    turn_y(f, NP - 1)

            def summary(b, more):
                if more:
                    turn_context(b + 1)
                attend(b, 0, 1)
                turn_a(b, NP - 1)
                if more:
                    context_bias(b + 1)
                batch_sum(b)
                attend(b, 1, 0)
                batch_cols(b)
                attend(b, 1, 1)

            pe.wait_ge(ident_rdy, 1)
            pe.wait_ge(ones_rdy, 1)
            pe.wait_ge(small_in, 16 * 5)
            pe.matmul(f_bank[0][:, 0:D + 3], ones[0:1, :], row[0:1, :], start=True, stop=True).then_inc(rows_ps, 1)
            turn_context(0)
            pe.wait_ge(w2b_rdy, KD)
            context_bias(0)
            scores(0, False)
            with pe.Fori(1, B) as b:
                summary(b - 1, True)
                scores(b, True)
            summary(B - 1, False)
            f = B - 1

            def turn_w(m):
                pe.wait_ge(wn_rdy, m + 1)
                if m == 0:
                    pe.wait_ge(hc_rdy, B)
                    pe.wait_ge(at_rdy, B * NP)
                if m == 2:
                    pe.wait_ge(pf_rdy, B * 4)
                    pe.wait_ge(x1_rdy, f * NP + 3)
                for q in range(3):
                    if m == 1:
                        pe.wait_ge(wt_rdy, q + 1)
                    for i in range(2):
                        for k in range(2):
                            at = (2 * q + i) * D + k * P if m < 2 else k * FF + (2 * q + i) * P
                            to = k * D + i * P if m < 2 else i * D + k * P
                            tr = pe.transpose(w_banks[m][q][:, to:to + P], wr[:, m, at:at + P], ident[:])
                    tr.then_inc(wt_ps, 1)

            for s in range(NP):
                project(f, s)
                if s >= 1:
                    turn_y(f, s - 1)
                if s < 2:
                    turn_w(s)
            turn_w(2)
            turn_y(f, NP - 1)

            def hidden(wh, wl, done, passed):
                with pe.Fori(0, KF) as k:
                    for hf in range(2):
                        pe.wait_ge(half_free[hf], k + 1 + done)
                        for q in range(4):
                            c = 4 * hf + q
                            if passed == 0:
                                pe.wait_ge(xh_rdy, c + 1)
                            n = slice(c * CH, (c + 1) * CH)
                            for d in range(KD):
                                for w_ in (wh, wl):
                                    pe.matmul(ps[hf][:, q, :], w_[:, d, ds(k * P, P)], xh[:, d, n],
                                              start=d == 0 and w_ is wh, stop=False)
                            if passed == 0:
                                pe.wait_ge(xq_rdy, c + 1)
                            for d in range(KD):
                                mm = pe.matmul(ps[hf][:, q, :], wh[:, d, ds(k * P, P)], xl[:, d, n],
                                               start=False, stop=d == KD - 1)
                        mm.then_inc(unit_ps, 1)

            pe.wait_ge(wt_rdy, 6)
            hidden(wgh, wgl, 0, 0)
            hidden(wuh, wul, KF, 1)
            hidden(wuh, wul, 2 * KF, 2)

            def down(c, par):
                pe.wait_ge(oh_rdy, c + 1)
                ge(pe, fin_rdy, c - 1)
                for low in (False, True):
                    if low:
                        pe.wait_ge(os_rdy, c + 1)
                    for t in range(CD // P):
                        q = slice(t * P, (t + 1) * P)
                        for k in range(KF):
                            for o_, w_ in ((ol, wdh),) if low else ((oh, wdh), (oh, wdl)):
                                mm = pe.matmul(ps[par][:, t, 0:D], o_[:, par, k, q], w_[:, k, :],
                                               start=not low and k == 0 and w_ is wdh, stop=low and k == KF - 1)
                mm.then_inc(dn_ps, 1)

            for i in range(SLOTS):
                if i < 2:
                    pe.wait_ge(half_free[i], 3 * KF + 1)
                down(i, i % 2)
            with pe.Fori(1, ND // SLOTS) as g:
                for i in range(SLOTS):
                    down(g * SLOTS + i, i % 2)

        @block.scalar
        def _(act):
            act.dma_start(row[0:1, 0:D], b_qv.rearrange("(a n) -> a n", a=1)).then_inc(small_in, 16)
            for n, s in enumerate((g_xattn, g_ffn, b_sim)):
                act.dma_start(row[0:1, D + n:D + n + 1], s.rearrange("(a n) -> a n", a=1)).then_inc(small_in, 16)
            act.dma_start(wcol[:], wsim_v, allow_slow_non_contiguous=True).then_inc(small_in, 16)
            act.preload_act_table(ACT.Exp)
            act.wait_ge(rows_ps, 1)
            act.activation(c_t2, f_bank[0][:, D:D + 2], ACT.Tanh).then_inc(tanh_rdy, 1)

            def turned_h(b, s):
                act.wait_ge(hT_ps, b * NP + s + 1)
                ge(act, pf_rdy, 4 * b)
                act.activation(hTf[:, :, s * PT:(s + 1) * PT], tb_bank.rearrange("p (d n) -> p d n", d=KD),
                               ACT.Copy).then_inc(hTf_rdy, 1)

            def high_h(b, s, proj):
                q = slice(s * PT, (s + 1) * PT)
                if proj:
                    act.wait_ge(f_ps, b * NP - NP + s + 1)
                act.wait_ge(hTf_rdy, b * NP + s + 1)
                act.activation(hth[:, :, q], hTf[:, :, q], ACT.Copy).then_inc(hth_rdy, 1)

            def turned_y(f, s):
                act.wait_ge(yT_ps, f * NP + s + 1)
                act.activation(yT[:, :, ds(f * S + s * PT, PT)], yb_bank.rearrange("p (d n) -> p d n", d=KD),
                               ACT.Copy).then_inc(yT_rdy, 1)

            def exps(b, s):
                act.wait_ge(nm_rdy, b * NP + s + 1)
                for t in range(2):
                    c = 2 * s + t
                    a_ = act.activation(sc[:, s % 2, t, :], sc[:, s % 2, t, :], ACT.Exp, bias=nm[:, c:c + 1],
                                        accum_out=rs[:, c:c + 1])
                a_.then_inc(exp_rdy, 1)

            def normed(b, s):
                act.wait_ge(ri_rdy, b * NP + s + 1)
                for t in range(2):
                    c = 2 * s + t
                    a_ = act.activation(sc[:, s % 2, t, :], sc[:, s % 2, t, :], ACT.Copy, scale=ri[:, c:c + 1])
                a_.then_inc(a_rdy, 1)

            def turned_a(b, s):
                act.wait_ge(at_ps, b * NP + s + 1)
                act.activation(ath[s // 2][0:JP, :, (s % 2) * PT:(s % 2 + 1) * PT],
                               ab_bank[0:JP, :].rearrange("p (k n) -> p k n", k=2), ACT.Copy).then_inc(ath_rdy, 1)

            def attended(b, hf, d):
                q = slice(hf * CH, (hf + 1) * CH)
                act.wait_ge(wml_rdy, 1)
                act.wait_ge(hq_ps, 4 * b + 2 * hf + d + 1)
                act.activation(hqh[:, d, q], hq_bank[d], ACT.Copy).then_inc(hqh_rdy, 1)

            def product(b, hf, d):
                q = slice(hf * CH, (hf + 1) * CH)
                act.wait_ge(pf_rdy, 4 * b + 2 * hf + d + 1)
                act.activation(prh[:, d, q], pf[:, d, :], ACT.Copy).then_inc(prh_rdy, 1)

            def turned_context(b):
                act.wait_ge(cxT_ps, b + 1)
                ge(act, cbi_ps, b)
                ge(act, cpf_rdy, b)
                act.activation(cxT[:], tb_bank[:, 0:2 * J].rearrange("p (d j) -> p d j", d=KD), ACT.Copy).then_inc(cxT_rdy, 1)

            def context_v(b):
                ge(act, hq_ps, 4 * b)
                act.wait_ge(cx_in, 16 * b + 16)
                act.activation(cxh[:], cx[:], ACT.Copy).then_inc(cxh_rdy, 1)

            def norm_x(b, s):
                act.wait_ge(nmr_rdy, b + 1)
                ge(act, hrow_ps, b)
                for t in range(2 * s, 2 * s + 2):
                    a_ = act.activation(h[:, t, :], xa[:, ds(b * TB + t, 1), :].rearrange("p a d -> p (a d)"), ACT.Identity,
                                        bias=nmr[:, t:t + 1], scale=rstd[:, t:t + 1])
                a_.then_inc(h_rdy, 1)

            def context_k(b):
                ge(act, cp_rdy, b)
                act.wait_ge(cxT_rdy, b + 1)
                for d in range(KD):
                    a_ = act.activation(cpf[:, d, :], cxT[:, d, :], ACT.Identity, bias=wcol[:, d:d + 1],
                                        scale=wcol[:, 2 * KD + d:2 * KD + d + 1])
                a_.then_inc(cpf_rdy, 1)
                act.wait_ge(cpf_rdy, b + 1)
                ge(act, sc_ps, NP * b)
                act.activation(cph[:], cpf[:], ACT.Copy).then_inc(cph_rdy, 1)

            def scores(b, proj):
                f = b - 1
                for s in range(NP):
                    if not proj and s == NP - 1:
                        act.wait_ge(wqv_in, 48)
                        act.activation(wmh[:], wmid[:], ACT.Copy).then_inc(wmh_rdy, 1)
                    if s == 0:
                        norm_x(b, 1)
                    turned_h(b, s)
                    high_h(b, s, proj)
                    if s >= 2:
                        turned_a(b, s - 2)
                    if 0 < s < NP - 1:
                        norm_x(b, s + 1)
                    if proj and s == NP - 1:
                        act.wait_ge(wqi_rdy, b)
                        act.activation(wr[:, ds(b - 1, 1), :].rearrange("p a n -> p (a n)"), wqi[:], ACT.Copy).then_inc(wqf_rdy, 1)
                    if s >= 1:
                        exps(b, s - 1)
                        normed(b, s - 1)
                    if proj and s >= 1:
                        turned_y(f, s - 1)
                exps(b, NP - 1)
                normed(b, NP - 1)
                act.wait_ge(ngm_rdy, b + 1)
                act.activation(eb, rm, ACT.Exp, bias=c_ngm, accum_out=c_es).then_inc(eb_rdy, 1)
                turned_a(b, NP - 2)
                attended(b, 0, 0)
                if proj:
                    turned_y(f, NP - 1)

            def summary(b, more):
                if more:
                    turned_context(b + 1)
                attended(b, 0, 1)
                turned_a(b, NP - 1)
                for d in range(KD):
                    product(b, 0, d)
                if more:
                    context_k(b + 1)
                attended(b, 1, 0)
                act.wait_ge(wef_rdy, b + 1)
                act.activation(weh[:], wef[:], ACT.Copy).then_inc(weh_rdy, 1)
                product(b, 1, 0)
                attended(b, 1, 1)
                if more:
                    norm_x(b + 1, 0)
                product(b, 1, 1)
                if more:
                    context_v(b + 1)

            turned_context(0)
            context_v(0)
            norm_x(0, 0)
            context_k(0)
            scores(0, False)
            with act.Fori(1, B) as b:
                summary(b - 1, True)
                scores(b, True)
            summary(B - 1, False)
            f = B - 1

            def turned_w(m):
                for q in range(3):
                    act.wait_ge(wt_ps, 3 * m + q + 1)
                    act.activation(w_part(m, q, 0), w_seen(m, q), ACT.Copy).then_inc(wth_rdy, 1)

            for s in range(NP):
                if s >= 1:
                    turned_y(f, s - 1)
                if s < 2:
                    turned_w(s)
            turned_w(2)
            turned_y(f, NP - 1)

            act.wait_ge(scales, 1)
            for c in range(NC):
                ge(act, xq_rdy, c - 1)
                act.activation(xqi[:, c % 2], yT[:, :, c * CH:(c + 1) * CH], ACT.Copy, scale=c_ix).then_inc(xqi_rdy, 1)
            act.wait_ge(x1_out, 16 * B)
            with act.Fori(0, KF) as k:
                for hf in range(2):
                    act.wait_ge(unit_ps, k * 2 + hf + 1)
                    act.activation(unit(hid, k, hf), ps_half(hf), ACT.Copy).then_inc(half_free[hf], 1)
            act.preload_act_table(ACT.Sigmoid)
            act.wait_ge(scales, 2)

            def gate_int(k, hf):
                act.activation(unit(gq, k, hf), unit(hid, k, hf), ACT.Copy, scale=c_cg).then_inc(gq_rdy, 1)

            def gate_abs(k, hf):
                ge(act, p_rdy, k * 2 + hf - 1)
                plain(act)
                act.activation(ag[:, hf, :], unit(hid, k, hf), ACT.Abs, scale=c_cg).then_inc(ag_rdy, 1)

            def gate_sigmoid(k, hf):
                u = k * 2 + hf
                act.wait_ge(gq_rdy, u + 1)
                act.wait_ge(ag_rdy, u + 1)
                plain(act)
                act.activation(unit(hid, k, hf), unit(gq, k, hf), ACT.Sigmoid, scale=c_sg).then_inc(sig_rdy, 1)

            def up_steps(k, hf):
                u = k * 2 + hf
                ge(act, o_rdy, u - 1)
                act.activation(pq[hf][:], unit(hid, k, hf), ACT.Copy, scale=c_cp).then_inc(pq_rdy, 1)
                act.wait_ge(unit_ps, 2 * NU + u + 1)
                plain(act)
                act.activation(au[:, hf, :], ps_half(hf), ACT.Abs, scale=c_cu).then_inc(au_rdy, 1)

            gate_int(0, 0)
            gate_abs(0, 0)
            gate_int(0, 1)
            gate_sigmoid(0, 0)
            gate_abs(0, 1)
            with act.Fori(1, KF) as k:
                gate_int(k, 0)
                gate_sigmoid(k - 1, 1)
                gate_abs(k, 0)
                gate_int(k, 1)
                gate_sigmoid(k, 0)
                gate_abs(k, 1)
            gate_sigmoid(KF - 1, 1)

            def first_up(u):
                act.wait_ge(scales, 3)
                act.wait_ge(unit_ps, 2 * NU + u + 1)
                act.wait_ge(p_rdy, NU - 1 + u)
                act.activation(au[:, u, :], ps_half(u), ACT.Abs, scale=c_cu).then_inc(au_rdy, 1)

            for u in range(2):
                first_up(u)
            act.wait_ge(scales, 4)
            for u in range(2):
                act.activation(pq[u][:], hid[:, 0, u * HALF:(u + 1) * HALF], ACT.Copy, scale=c_cp).then_inc(pq_rdy, 1)
            with act.Fori(1, KF) as k:
                for hf in range(2):
                    up_steps(k, hf)
            act.wait_ge(scales, 5)

            def product_q(c, par):
                ge(act, os_rdy, c - 1)
                act.activation(oq[:, par], hid[:, :, ds(c * CD, CD)], ACT.Copy, scale=c_co).then_inc(oqa_rdy, 1)

            for i in range(SLOTS):
                product_q(i, i % 2)
            with act.Fori(1, ND // SLOTS) as g:
                for i in range(SLOTS):
                    product_q(g * SLOTS + i, i % 2)

        @block.vector
        def _(dve):
            done = [0]

            def link(ins):
                done[0] += 1
                ins.then_inc(chain, 1)
                dve.wait_ge(chain, done[0])

            def stats(b, lo, hi):
                if lo == 0:
                    ge(dve, mv_done, b)
                for t in range(lo, hi):
                    i_ = dve.bn_stats(st[:, t, :], xa[:, ds(b * TB + t, 1), :].rearrange("p a d -> p (a d)"))
                i_.then_inc(bn_done, 1)

            def row_stats(b):
                ge(dve, h_rdy, b * NP)
                dve.wait_ge(bn_done, 2 * b + 2)
                plain(dve)
                for t in range(TB):
                    i_ = dve.bn_aggr(mv[:, t, :], st[:, t, :])
                i_.then_inc(mv_done, 1)
                dve.wait_ge(mv_done, b + 1)
                dve.tensor_scalar(rstd, mv[:, :, 1], LN_EPS, None, ALU.add).then_inc(vp_done, 1)

            def row_shift(b):
                dve.wait_ge(rstd_rdy, b + 1)
                dve.scalar_tensor_tensor(nmr, mv[:, :, 0], -1.0, rstd, ALU.mult, ALU.mult).then_inc(nmr_rdy, 1)

            def context_bias(b):
                dve.wait_ge(cbi_ps, b + 1)
                dve.tensor_scalar(cbi[:], tb_bank[:, 2 * J:3 * J], c_bs, None, ALU.add).then_inc(cbi_rdy, 1)

            def scored(b, s):
                n = b * NP + s
                dve.wait_ge(sc_ps, n + 1)
                dve.wait_ge(cbi_rdy, b + 1)
                ge(dve, at_ps, n - 1)
                plain(dve)
                for t in range(2):
                    i_ = dve.tensor_tensor_reduce(sc[:, s % 2, t, :], s_bank[s % 2][:, t * J:(t + 1) * J], cbi[:], 1.0,
                                                  -3.4e38, ALU.add, ALU.max, rm[:, 2 * s + t:2 * s + t + 1])
                i_.then_inc(sc_rdy, 1)
                dve.wait_ge(sc_rdy, n + 1)
                dve.tensor_scalar(nm[:, 2 * s:2 * s + 2], rm[:, 2 * s:2 * s + 2], -1.0, None, ALU.mult).then_inc(nm_rdy, 1)

            def normed(b, s):
                dve.wait_ge(exp_rdy, b * NP + s + 1)
                dve.reciprocal(ri[:, 2 * s:2 * s + 2], rs[:, 2 * s:2 * s + 2]).then_inc(ri_rdy, 1)

            def turned_a(b, s):
                dve.wait_ge(ath_rdy, b * NP + s + 1)
                q = slice((s % 2) * PT, (s % 2 + 1) * PT)
                dve.tensor_tensor(atl[s // 2][0:JP, :, q], ab_bank[0:JP, :].rearrange("p (k n) -> p k n", k=2),
                                  ath[s // 2][0:JP, :, q].bitcast(F32), ALU.subtract).then_inc(at_rdy, 1)

            def attended(b, hf, d):
                q = slice(hf * CH, (hf + 1) * CH)
                n = b * 4 + hf * 2 + d
                dve.wait_ge(hqh_rdy, n + 1)
                dve.tensor_tensor(hql[:, d, q], hq_bank[d], hqh[:, d, q].bitcast(F32), ALU.subtract).then_inc(hql_rdy, 1)
                if hf == 1:
                    dve.wait_ge(prl_rdy, n - 1)
                dve.tensor_tensor(pf[:, d, :], hq_bank[d], hTf[:, d, q], ALU.mult).then_inc(pf_rdy, 1)

            def residual(f, s):
                n = f * NP + s
                g = f * TB + 2 * s
                dve.wait_ge(f_ps, n + 1)
                dve.wait_ge(xb_rdy, n + 1)
                x_ = xa[:, ds(g, 2), :]
                dve.scalar_tensor_tensor(x_, f_bank[s % 2].rearrange("p (t d) -> p t d", t=2), c_tx, x_,
                                         ALU.mult, ALU.add).then_inc(x1_rdy, 1)
                dve.wait_ge(x1_rdy, n + 1)
                plain(dve)
                for t in range(2):
                    i_ = dve.bn_stats(st[:, t, :], xa[:, ds(g + t, 1), :].rearrange("p a d -> p (a d)"))
                i_.then_inc(bn2_done, 1)
                dve.wait_ge(bn2_done, n + 1)
                plain(dve)
                for t in range(2):
                    i_ = dve.bn_aggr(mv2[:, t, :], st[:, t, :])
                i_.then_inc(mv2_done, 1)
                dve.wait_ge(mv2_done, n + 1)
                dve.tensor_scalar(vp2, mv2[:, :, 1], LN_EPS, None, ALU.add).then_inc(vp2_done, 1)

            def norm_x1(f, s):
                n = f * NP + s
                dve.wait_ge(rstd2_rdy, n + 1)
                if s >= 2:
                    dve.wait_ge(yT_ps, f * NP + s - 1)
                for t in range(2):
                    i_ = dve.tensor_scalar(yb[:, s % 2, t, :], xa[:, ds(f * TB + 2 * s + t, 1), :].rearrange("p a d -> p (a d)"),
                                           mv2[:, t, 0:1], rstd2[:, t:t + 1], ALU.subtract, ALU.mult)
                i_.then_inc(y_rdy, 1)

            def max_y(f, s):
                n = f * NP + s
                dve.wait_ge(y_rdy, n + 1)
                dve.tensor_reduce(ymx[:, ds(n, 1)], yb[:, s % 2].rearrange("p t d -> p (t d)"), AX.X, ALU.max,
                                  apply_absolute_value=True).then_inc(ym_done, 1)

            WL = 7

            def wlink(m, i, ins):
                ins.then_inc(wchain, 1)
                dve.wait_ge(wchain, m * WL + i + 1)

            def weight_scales(m):
                wlink(m, 0, dve.tensor_reduce(wsc[:], wr[:, ds(m, 1), :].rearrange("p a (n k) -> p (a n) k", k=QB),
                                              AX.X, ALU.max, apply_absolute_value=True))
                wlink(m, 1, dve.tensor_scalar(wsc[:], wsc[:], 1.0 / 7.0, EPS, ALU.mult, ALU.max))
                wlink(m, 2, dve.tensor_reduce(c_sm, wsc[:], AX.X, ALU.max))
                dve.reciprocal(wri[:], wsc[:]).then_inc(wmax_rdy, 1)

            def weight_unit(m):
                dve.wait_ge(wall_rdy, m + 1)
                wlink(m, 3, dve.tensor_scalar(c_pw.bitcast(I32), c_sa.bitcast(I32), 0x7F800000, None, ALU.bitwise_and))
                wlink(m, 4, dve.reciprocal(c_wt, c_pw))
                wlink(m, 5, dve.tensor_scalar(c_dn[:, ds(m, 1)], c_pw, 1.0 / W_SCALE, None, ALU.mult))
                wlink(m, 6, dve.tensor_scalar(wsc[:], wsc[:], c_wt, W_SCALE, ALU.mult, ALU.mult))

            def weight_values(m):
                dve.wait_ge(wq_rdy, 2 * m + 2)
                wm = wr[:, ds(m, 1), :].rearrange("p a n -> p (a n)")
                dve.tensor_scalar(wqi[:], wm, 7.0, -8.0, ALU.min, ALU.max).then_inc(wqi_rdy, 1)

            def weight_parts(m):
                for q in range(3):
                    dve.wait_ge(wth_rdy, 3 * m + q + 1)
                    dve.tensor_tensor(w_part(m, q, 1), w_seen(m, q), w_part(m, q, 0), ALU.subtract).then_inc(wt_rdy, 1)

            def scores(b, proj):
                f = b - 1
                for s in range(NP):
                    if proj:
                        residual(f, s)
                    elif s == NP - 1:
                        dve.wait_ge(wmh_rdy, 1)
                        dve.tensor_tensor(wml[:], wmid[:], wmh[:].bitcast(F32), ALU.subtract).then_inc(wml_rdy, 1)
                    if s >= 2:
                        turned_a(b, s - 2)
                    if s >= 1:
                        scored(b, s - 1)
                    if proj:
                        norm_x1(f, s)
                    if s >= 1:
                        normed(b, s - 1)
                    if proj:
                        max_y(f, s)
                        if s == 1:
                            weight_unit(b - 1)
                        if s == 2:
                            weight_values(b - 1)
                scored(b, NP - 1)
                dve.tensor_reduce(c_m1, rm, AX.X, ALU.max).then_inc(m1_rdy, 1)
                dve.wait_ge(m1_rdy, b + 1)
                dve.tensor_scalar(diag[:], ident[:], c_m1, None, ALU.mult).then_inc(diag_rdy, 1)
                normed(b, NP - 1)
                dve.wait_ge(m_ps, b + 1)
                dve.tensor_reduce(c_ngm, sb_bank[:, 0:P], AX.X, ALU.max, negate=True).then_inc(ngm_rdy, 1)
                turned_a(b, NP - 2)
                attended(b, 0, 0)

            def summary(b, more):
                if more:
                    stats(b + 1, 0, TB // 2)
                attended(b, 0, 1)
                turned_a(b, NP - 1)
                if more:
                    context_bias(b + 1)
                dve.wait_ge(hrow_ps, b + 1)
                dve.reciprocal(c_rs, sb_bank[:, SUM:SUM + 1]).then_inc(crs_rdy, 1)
                dve.tensor_copy(hrow[0:1, :], sb_bank[0:1, P:P + D]).then_inc(hrow_rdy, 1)
                if more:
                    stats(b + 1, TB // 2, TB)
                dve.wait_ge(crs_rdy, b + 1)
                dve.wait_ge(hc_ps, b + 1)
                dve.tensor_scalar(c_hc, sb_bank[:, SUM + 1:SUM + 1 + KD], c_rs, None, ALU.mult).then_inc(hc_rdy, 1)
                dve.wait_ge(hc_rdy, b + 1)
                for d in range(KD):
                    i_ = dve.scalar_tensor_tensor(wef[:, d, :], w3[:, d, :], c_hc[:, d:d + 1], w0[:, d, :], ALU.mult, ALU.add)
                i_.then_inc(wef_rdy, 1)
                if more:
                    row_stats(b + 1)
                dve.wait_ge(weh_rdy, b + 1)
                dve.tensor_tensor(wel[:], wef[:], weh[:].bitcast(F32), ALU.subtract).then_inc(we_rdy, 1)
                attended(b, 1, 0)
                if more:
                    row_shift(b + 1)
                attended(b, 1, 1)
                if more:
                    weight_scales(b)

            dve.wait_ge(x0_in, 16 * NP)
            stats(0, 0, TB // 2)
            stats(0, TB // 2, TB)
            row_stats(0)
            dve.wait_ge(ones_rdy, 1)
            dve.wait_ge(small_in, 80)
            for d in range(KD):
                dve.tensor_scalar(w2b[:, d, :], ones[:], wcol[:, KD + d:KD + d + 1], None, ALU.mult).then_inc(w2b_rdy, 1)
            dve.wait_ge(ident_rdy, 1)
            dve.wait_ge(tanh_rdy, 1)
            link(dve.tensor_copy(c_bs, f_bank[0][:, D + 2:D + 3]))
            context_bias(0)
            row_shift(0)
            dve.tensor_scalar(tgb[:], f_bank[0][:, 0:D], c_tx, None, ALU.mult).then_inc(tgb_rdy, 1)
            scores(0, False)
            dve.wait_ge(xr_in, 16 * (B - 1))
            dve.wait_ge(wffn_in, 48)
            with dve.Fori(1, B) as b:
                summary(b - 1, True)
                scores(b, True)
            summary(B - 1, False)
            f = B - 1
            for s in range(NP):
                residual(f, s)
                if s >= 1:
                    max_y(f, s - 1)
                norm_x1(f, s)
                if s < 2:
                    weight_parts(s)
            max_y(f, NP - 1)

            def largest(n, counts, m):
                dve.wait_ge(*counts)
                dve.tensor_reduce(c_loc[:, n:n + 1], m, AX.X, ALU.max).then_inc(loc_rdy, 1)

            def overall(n):
                dve.wait_ge(all_rdy, n + 1)
                return c_all[:, n:n + 1]

            largest(0, (ym_done, B * NP), ymx)
            v = overall(0)
            link(dve.tensor_scalar(c_sx, v, 1.0 / QMAX, EPS, ALU.mult, ALU.max))
            dve.reciprocal(c_ix, c_sx).then_inc(scales, 1)
            dve.wait_ge(yT_rdy, B * NP)
            dve.tensor_scalar(c_kg, c_sx, c_dn[:, 0:1], None, ALU.mult).then_inc(half_free[0], 1)
            for c in range(NC):
                if c == NC // 2:
                    weight_parts(2)
                    dve.tensor_scalar(c_ku, c_sx, c_dn[:, 1:2], None, ALU.mult).then_inc(half_free[1], 1)
                dve.wait_ge(xqi_rdy, c + 1)
                n = slice(c * CH, (c + 1) * CH)
                dve.tensor_copy(xh[:, :, n], xqi[:, c % 2]).then_inc(xh_rdy, 1)
                dve.wait_ge(xh_rdy, c + 1)
                dve.tensor_tensor(xl[:, :, n], xqi[:, c % 2], xh[:, :, n], ALU.subtract).then_inc(xq_rdy, 1)
            dve.wait_ge(half_free[0], 1)
            dve.wait_ge(half_free[1], 1)
            dve.tensor_scalar(c_kgq, c_kg, 1.0 / QMAX, None, ALU.mult)
            dve.tensor_scalar(c_kuq, c_ku, 1.0 / QMAX, None, ALU.mult)
            link(dve.tensor_scalar(c_ft, c_tf, c_dn[:, 2:3], None, ALU.mult))
            with dve.Fori(0, KF) as k:
                for hf in range(2):
                    dve.wait_ge(half_free[hf], k + 2)
                    dve.tensor_reduce(gmx[:, ds(k * 2 + hf, 1)], unit(hid, k, hf), AX.X, ALU.max,
                                      apply_absolute_value=True).then_inc(gm_done, 1)
            largest(1, (gm_done, NU), gmx)
            v = overall(1)
            link(dve.tensor_scalar(c_sg, v, c_kgq, EPS, ALU.mult, ALU.max))
            link(dve.reciprocal(c_rg, c_sg))
            dve.tensor_scalar(c_cg, c_rg, c_kg, None, ALU.mult).then_inc(scales, 1)
            link(dve.tensor_scalar(c_kp, c_sg, 1.0 / 65536.0, None, ALU.mult))
            link(dve.tensor_scalar(c_kpq, c_kp, 1.0 / QMAX, None, ALU.mult))

            def up_max(u):
                dve.wait_ge(unit_ps, NU + u + 1)
                dve.tensor_reduce(umx[:, u:u + 1], ps_half(u % 2), AX.X, ALU.max,
                                  apply_absolute_value=True).then_inc(half_free[u % 2], 1)

            def gated(u):
                k, hf = u // 2, u % 2
                dve.wait_ge(sig_rdy, u + 1)
                ge(dve, p_rdy, u)
                dve.tensor_scalar(sq[:], hid[:, k, hf * HALF:(hf + 1) * HALF], 65536.0, None, ALU.mult).then_inc(sq_rdy, 1)

            def gated_max(u):
                k, hf = u // 2, u % 2
                dve.wait_ge(sq_rdy, u + 1)
                dve.wait_ge(ag_rdy, u + 1)
                dve.tensor_tensor_reduce(hid[:, k, hf * HALF:(hf + 1) * HALF], ag[:, hf, :], sq[:], 1.0, 0.0,
                                         ALU.mult, ALU.max, pmx[:, u:u + 1]).then_inc(p_rdy, 1)

            up_max(0)
            up_max(1)
            for u in range(NU):
                gated(u)
                if u + 2 < NU:
                    up_max(u + 2)
                if u == NU - 2:
                    v = overall(2)
                    link(dve.tensor_scalar(c_su, v, c_kuq, EPS, ALU.mult, ALU.max))
                    link(dve.reciprocal(c_ru, c_su))
                    dve.tensor_scalar(c_cu, c_ru, c_ku, None, ALU.mult).then_inc(scales, 1)
                gated_max(u)
                if u == NU - 3:
                    dve.wait_ge(half_free[1], 2 * KF + 1)
                    largest(2, (half_free[0], 2 * KF + 1), umx)
            largest(3, (p_rdy, NU), pmx)

            def product_sign(u):
                k, hf = u // 2, u % 2
                g_ = gq[:, k, hf * HALF:(hf + 1) * HALF]
                dve.wait_ge(au_rdy, u + 1)
                dve.tensor_tensor(g_.bitcast(BF16), g_, ps_half(hf), ALU.mult).then_inc(half_free[hf], 1)

            def product_max(u):
                k, hf = u // 2, u % 2
                dve.wait_ge(au_rdy, u + 1)
                dve.wait_ge(pq_rdy, u + 1)
                dve.tensor_tensor_reduce(hid[:, k, hf * HALF:(hf + 1) * HALF], pq[hf][:], au[:, hf, :], 1.0, 0.0,
                                         ALU.mult, ALU.max, omx[:, u:u + 1]).then_inc(o_rdy, 1)

            product_sign(0)
            v = overall(3)
            link(dve.tensor_scalar(c_sp, v, c_kpq, EPS, ALU.mult, ALU.max))
            link(dve.reciprocal(c_rp, c_sp))
            dve.tensor_scalar(c_cp, c_rp, c_kp, None, ALU.mult).then_inc(scales, 1)
            link(dve.tensor_scalar(c_ko, c_su, c_sp, None, ALU.mult))
            for u in range(NU):
                if 0 < u < NU - 1:
                    product_sign(u)
                product_max(u)
            largest(4, (o_rdy, NU), omx)
            v = overall(4)
            link(dve.tensor_scalar(c_so, v, c_ko, 1.0 / QMAX, ALU.mult, ALU.mult))
            link(dve.tensor_scalar(c_so, c_so, EPS, None, ALU.max))
            link(dve.reciprocal(c_ro, c_so))
            dve.tensor_scalar(c_co, c_ro, c_ko, None, ALU.mult).then_inc(scales, 1)
            link(dve.tensor_scalar(c_fin, c_so, c_ft, None, ALU.mult))
            dve.wait_ge(half_free[0], 3 * KF + 1)

            def signed(c, par):
                sg = gq[:, :, ds(c * CD, CD)].bitcast(BF16)
                dve.tensor_scalar(sg, sg, 1.0, -1.0, ALU.min, ALU.max).then_inc(sgn_rdy, 1)
                dve.wait_ge(oqa_rdy, c + 1)
                dve.wait_ge(sgn_rdy, c + 1)
                dve.tensor_tensor(oq[:, par], oq[:, par], sg, ALU.mult).then_inc(oqs_rdy, 1)
                dve.wait_ge(oqs_rdy, c + 1)
                ge(dve, dn_ps, c - 1)
                dve.tensor_copy(oh[:, par], oq[:, par]).then_inc(oh_rdy, 1)
                dve.wait_ge(oh_rdy, c + 1)
                dve.tensor_tensor(ol[:, par], oq[:, par], oh[:, par], ALU.subtract).then_inc(os_rdy, 1)

            def final(g, i):
                dve.wait_ge(dn_ps, g * SLOTS + i + 1)
                dve.wait_ge(xo_in[i], g * 16 + 16)
                y_ = xo[:, i]
                dve.scalar_tensor_tensor(y_, ps[i % 2][:, 0:CD // P, 0:D], c_fin, y_, ALU.mult, ALU.add).then_inc(fin_rdy, 1)

            for i in range(SLOTS):
                signed(i, i % 2)
                if i == 0:
                    product_sign(NU - 1)
                    dve.wait_ge(half_free[1], 3 * KF + 1)
                if i >= 1:
                    final(0, i - 1)
            with dve.Fori(1, ND // SLOTS) as g:
                for i in range(SLOTS):
                    signed(g * SLOTS + i, i % 2)
                    if i == 0:
                        final(g - 1, SLOTS - 1)
                    else:
                        final(g, i - 1)
            final(ND // SLOTS - 1, SLOTS - 1)


_INS = ["x", "ctx_1024", "g_xattn", "g_ffn", "L0_xattn_w_sim", "L0_xattn_b_sim", "L0_xattn_W_qv", "L0_xattn_b_qv",
        "L0_ffn_w_gate", "L0_ffn_w_up", "L0_ffn_w_down"]


def kernel(**inputs):
    import numpy as _np
    import concourse.bacc as _bacc
    from concourse.bass_utils import run_bass_kernel_spmd as _run

    nc = _bacc.Bacc("TRN2", target_bir_lowering=False, num_devices=1)
    arrays, args = {}, []
    for name in _INS:
        v = _np.ascontiguousarray(inputs[name])
        arrays[f"in_{name}"] = v
        args.append(nc.dram_tensor(f"in_{name}", v.shape, mybir.dt.from_np(v.dtype), kind="ExternalInput").ap())
    out = nc.dram_tensor("out_dram", (B, S, D), F32, kind="ExternalOutput").ap()
    build(nc, *args, out)
    r = _run(nc, [arrays], core_ids=[0])
    return r.results[0]["out_dram"]
```
